# Optimizing a Trainium2 kernel written in Bass

```python
import numpy as np
import jax
import jax.numpy as jnp

def _softmax(x, axis=-1):
    return jax.nn.softmax(x, axis=axis)

def _gelu(x):
    return jax.nn.gelu(x, approximate=True)

def _silu(x):
    return jax.nn.silu(x)

def _sigmoid(x):
    return jax.nn.sigmoid(x)

def _layernorm(x, axis=-1, eps=1e-05):
    m = jnp.mean(x, axis=axis, keepdims=True)
    v = jnp.var(x, axis=axis, keepdims=True)
    return (x - m) / jnp.sqrt(v + eps)

def _scatter_add(tgt, idx, src, axis=0):
    return tgt.at[idx].add(src)

def _segment_sum(src, seg, n):
    return jax.ops.segment_sum(src, seg, n)
kernel_name = 'mk_macaron_d1_jaxref_r4_b155b3'

def setup_inputs(seed: int=0):
    np.random.seed(seed)
    _w = jnp.asarray

    def _L0_attn_setup():
        import jax, jax.numpy as jnp
        import numpy as np
        E = 256
        H = 16
        D = E // H
        K = 4
        MAX_SEQ = 2048
        ROPE_BASE = 10000.0
        SCALE = D ** (-0.5)

        def rotate_half(x):
            half = x.shape[-1] // 2
            return jnp.concatenate([-x[..., half:], x[..., :half]], axis=-1)

        def _rope_cache():
            inv_freq = 1.0 / ROPE_BASE ** (jnp.arange(0, D, 2, dtype=jnp.float32) / D)
            t = jnp.arange(MAX_SEQ, dtype=jnp.float32)
            freqs = jnp.outer(t, inv_freq)
            emb = jnp.concatenate([freqs, freqs], axis=-1)
            return (jnp.cos(emb), jnp.sin(emb))
        key = jax.random.key(seed)
        ks = jax.random.split(key, 6)
        B, S = (2, 512)
        w_scale = E ** (-0.5)
        return {'x': jax.random.normal(ks[0], (B, S, E), dtype=jnp.float32), 'Wq': jax.random.normal(ks[1], (E, E), dtype=jnp.float32) * w_scale, 'Wk': jax.random.normal(ks[2], (E, E), dtype=jnp.float32) * w_scale, 'Wv': jax.random.normal(ks[3], (E, E), dtype=jnp.float32) * w_scale, 'Wr': jax.random.normal(ks[4], (E, H * K), dtype=jnp.float32) * w_scale, 'Wo': jax.random.normal(ks[5], (E, E), dtype=jnp.float32) * w_scale}
    _L0_attn_in = _L0_attn_setup()

    def _L0_ffn_setup():
        import math
        import jax, jax.numpy as jnp
        import numpy as np
        D_MODEL = 256
        NUM_EXPERTS = 8
        D_FF_EXPERT = max(64, int(D_MODEL * 4 * 0.25))
        THRESHOLD = 0.9
        CAP_FACTOR = 1.0
        INIT_STD = 0.02

        def _xmoe_route(probs):
            N, E = probs.shape
            order = jnp.argsort(-probs, axis=-1)
            p_sorted = jnp.take_along_axis(probs, order, axis=-1)
            csum = jnp.cumsum(p_sorted, axis=-1)
            reached = (csum >= THRESHOLD).at[:, -1].set(True)
            k_idx = jnp.argmax(reached, axis=-1)
            select_prefix = jnp.arange(E)[None, :] <= k_idx[:, None]
            rows = jnp.arange(N)[:, None]
            assign_mask = jnp.zeros((N, E), dtype=bool).at[rows, order].set(select_prefix)
            rank = jnp.arange(1, E + 1, dtype=probs.dtype)[None, :]
            R_sorted = jnp.where(select_prefix, p_sorted - rank, jnp.full_like(p_sorted, -1000000000.0))
            R = jnp.zeros((N, E), dtype=probs.dtype).at[rows, order].set(R_sorted)
            capacity = int(math.ceil(N / E) * CAP_FACTOR)
            C = min(capacity, N)
            tok_order = jnp.argsort(-R, axis=0)
            topC = tok_order[:C, :]
            keep = jnp.zeros((N, E), dtype=bool).at[topC, jnp.arange(E)[None, :]].set(True)
            final_mask = assign_mask & keep
            return jnp.where(final_mask, probs, jnp.zeros_like(probs))
        key = jax.random.key(seed)
        k_x, k_g, k_w1, k_w2 = jax.random.split(key, 4)
        B, T = (4, 512)
        x = jax.random.normal(k_x, (B, T, D_MODEL), dtype=jnp.float32)
        bound = 1.0 / math.sqrt(D_MODEL)
        gate_w = jax.random.uniform(k_g, (NUM_EXPERTS, D_MODEL), minval=-bound, maxval=bound, dtype=jnp.float32)
        w1 = INIT_STD * jax.random.normal(k_w1, (NUM_EXPERTS, D_FF_EXPERT, D_MODEL), dtype=jnp.float32)
        w2 = INIT_STD * jax.random.normal(k_w2, (NUM_EXPERTS, D_MODEL, D_FF_EXPERT), dtype=jnp.float32)
        return {'x': x, 'gate_w': gate_w, 'w1': w1, 'w2': w2}
    _L0_ffn_in = _L0_ffn_setup()
    _d = {'L0_attn_x': _L0_attn_in['x'], 'L0_attn_Wq': _L0_attn_in['Wq'], 'L0_attn_Wk': _L0_attn_in['Wk'], 'L0_attn_Wv': _L0_attn_in['Wv'], 'L0_attn_Wr': _L0_attn_in['Wr'], 'L0_attn_Wo': _L0_attn_in['Wo'], 'L0_ffn_gate_w': _L0_ffn_in['gate_w'], 'L0_ffn_w1': _L0_ffn_in['w1'], 'L0_ffn_w2': _L0_ffn_in['w2']}
    _x0 = _d['L0_attn_x']
    _d['L0_attn_x'] = jax.random.normal(jax.random.fold_in(jax.random.key(seed), 1), (4, 2048, 256), dtype=_x0.dtype)
    del _x0
    return _d

def reference(L0_attn_x, L0_attn_Wq, L0_attn_Wk, L0_attn_Wv, L0_attn_Wr, L0_attn_Wo, L0_ffn_gate_w, L0_ffn_w1, L0_ffn_w2):

    def _L0_attn_ref(x, Wq, Wk, Wv, Wr, Wo):
        import jax, jax.numpy as jnp
        import numpy as np
        E = 256
        H = 16
        D = E // H
        K = 4
        MAX_SEQ = 2048
        ROPE_BASE = 10000.0
        SCALE = D ** (-0.5)

        def rotate_half(x):
            half = x.shape[-1] // 2
            return jnp.concatenate([-x[..., half:], x[..., :half]], axis=-1)

        def _rope_cache():
            inv_freq = 1.0 / ROPE_BASE ** (jnp.arange(0, D, 2, dtype=jnp.float32) / D)
            t = jnp.arange(MAX_SEQ, dtype=jnp.float32)
            freqs = jnp.outer(t, inv_freq)
            emb = jnp.concatenate([freqs, freqs], axis=-1)
            return (jnp.cos(emb), jnp.sin(emb))
        B, S, _ = x.shape
        q = (x @ Wq).reshape(B, S, H, D).transpose(0, 2, 1, 3)
        k = (x @ Wk).reshape(B, S, H, D).transpose(0, 2, 1, 3)
        v = (x @ Wv).reshape(B, S, H, D).transpose(0, 2, 1, 3)
        logits = (x @ Wr).reshape(B, S, H, K).transpose(0, 2, 1, 3)
        node_probs = jax.nn.softmax(logits, axis=-1)
        expected_pos = jnp.cumsum(node_probs, axis=2) - node_probs
        cos_c, sin_c = _rope_cache()
        pos = jnp.clip(expected_pos, 0.0, MAX_SEQ - 1)
        pf = pos.astype(jnp.int32)
        pc = jnp.minimum(pf + 1, MAX_SEQ - 1)
        frac = (pos - pf.astype(pos.dtype))[..., None]
        cos = cos_c[pf] + frac * (cos_c[pc] - cos_c[pf])
        sin = sin_c[pf] + frac * (sin_c[pc] - sin_c[pf])
        cos_w = jnp.einsum('bhsk,bhskd->bhsd', node_probs, cos)
        sin_w = jnp.einsum('bhsk,bhskd->bhsd', node_probs, sin)
        q_r = q * cos_w + rotate_half(q) * sin_w
        k_r = k * cos_w + rotate_half(k) * sin_w
        node_w = jnp.einsum('bhik,bhjk->bhij', node_probs, node_probs)
        scores = jnp.einsum('bhid,bhjd->bhij', q_r, k_r) * SCALE
        scores = scores + jnp.log(node_w + 1e-08)
        causal = jnp.tril(jnp.ones((S, S), dtype=bool))
        scores = jnp.where(causal[None, None], scores, -jnp.inf)
        attn = jax.nn.softmax(scores, axis=-1)
        out = jnp.einsum('bhij,bhjd->bhid', attn, v)
        out = out.transpose(0, 2, 1, 3).reshape(B, S, E)
        return out @ Wo

    def _L0_ffn_ref(x, gate_w, w1, w2):
        import math
        import jax, jax.numpy as jnp
        import numpy as np
        D_MODEL = 256
        NUM_EXPERTS = 8
        D_FF_EXPERT = max(64, int(D_MODEL * 4 * 0.25))
        THRESHOLD = 0.9
        CAP_FACTOR = 1.0
        INIT_STD = 0.02

        def _xmoe_route(probs):
            N, E = probs.shape
            order = jnp.argsort(-probs, axis=-1)
            p_sorted = jnp.take_along_axis(probs, order, axis=-1)
            csum = jnp.cumsum(p_sorted, axis=-1)
            reached = (csum >= THRESHOLD).at[:, -1].set(True)
            k_idx = jnp.argmax(reached, axis=-1)
            select_prefix = jnp.arange(E)[None, :] <= k_idx[:, None]
            rows = jnp.arange(N)[:, None]
            assign_mask = jnp.zeros((N, E), dtype=bool).at[rows, order].set(select_prefix)
            rank = jnp.arange(1, E + 1, dtype=probs.dtype)[None, :]
            R_sorted = jnp.where(select_prefix, p_sorted - rank, jnp.full_like(p_sorted, -1000000000.0))
            R = jnp.zeros((N, E), dtype=probs.dtype).at[rows, order].set(R_sorted)
            capacity = int(math.ceil(N / E) * CAP_FACTOR)
            C = min(capacity, N)
            tok_order = jnp.argsort(-R, axis=0)
            topC = tok_order[:C, :]
            keep = jnp.zeros((N, E), dtype=bool).at[topC, jnp.arange(E)[None, :]].set(True)
            final_mask = assign_mask & keep
            return jnp.where(final_mask, probs, jnp.zeros_like(probs))
        B, T, D = x.shape
        N = B * T
        xf = x.reshape(N, D)
        probs = jax.nn.softmax(xf @ gate_w.T, axis=-1)
        scores_sel = _xmoe_route(probs)
        h = jax.nn.gelu(jnp.einsum('nd,efd->enf', xf, w1), approximate=False)
        y_e = jnp.einsum('enf,edf->end', h, w2)
        y = jnp.einsum('ne,end->nd', scores_sel, y_e)
        return y.reshape(B, T, D)
    x = L0_attn_x
    x = x + 0.5 * _L0_ffn_ref(_layernorm(x, axis=-1), L0_ffn_gate_w, L0_ffn_w1, L0_ffn_w2)
    x = x + _L0_attn_ref(_layernorm(x, axis=-1), L0_attn_Wq, L0_attn_Wk, L0_attn_Wv, L0_attn_Wr, L0_attn_Wo)
    x = x + 0.5 * _L0_ffn_ref(_layernorm(x, axis=-1), L0_ffn_gate_w, L0_ffn_w1, L0_ffn_w2)
    return x

_drawn_inputs = setup_inputs


def setup_inputs(seed=0):
    import zlib

    import numpy as np

    out = dict(_drawn_inputs(seed))
    spreads = {}
    factors = {'L0_ffn_gate_w': 4.147, 'L0_ffn_w1': 3.983, 'L0_ffn_w2': 3.862}
    for name, (base, spread) in spreads.items():
        noise = np.random.default_rng([zlib.crc32(name.encode()), seed]).standard_normal(out[name].shape)
        drawn = base * np.exp(spread * noise) if base else spread * noise
        out[name] = jnp.asarray(drawn.astype(out[name].dtype))
    for name, factor in factors.items():
        out[name] = (out[name] * factor).astype(out[name].dtype)
    return out
```

```python
import concourse.bass as bass
from concourse import mybir
from contextlib import ExitStack

import numpy as np

F32 = mybir.dt.float32
BF16 = mybir.dt.bfloat16
I32 = mybir.dt.int32
ALU = mybir.AluOpType
ACT = mybir.ActivationFunctionType
AX = mybir.AxisListType

P = 128
D = 256
DK = D // P
LN_EPS = 1e-5


class Chain:

    def __init__(self, eng, sem):
        self.eng, self.sem, self.base, self.n = eng, sem, 0, 0

    def __call__(self, ins):
        self.add(ins)
        self.wait()

    def add(self, ins):
        ins.then_inc(self.sem, 1)
        self.n += 1

    def wait(self):
        self.eng.wait_ge(self.sem, self.base + self.n)

    def at(self, start, i, per):
        self.base, self.n = start + i * per, 0

    def after(self, start, count, per):
        assert self.n == per, (self.n, per)
        self.base, self.n = start + count * per, 0


def identity(pool, chain, tile, n=P):
    chain(pool.memset(tile, 0.0))
    chain(pool.affine_select(out=tile, in_=tile, compare_op=ALU.not_equal, fill=1.0,
                             base=0, pattern=[[-1, n]], channel_multiplier=1))


def build_ffn(nc, name, src, dst, residual, gate_w, w1, w2, table):
    N = src.shape[0]
    T = N // P
    NE, F, _ = w1.shape
    FK = F // P
    CAP = -(-N // NE)
    J = CAP // P
    SLOT_LO = 32
    SLOT_HI = CAP // SLOT_LO
    ROW = table.shape[1]
    GT = 4
    G = T // GT
    THRESHOLD = 0.9
    NOT_CHOSEN = -16.0
    SEARCH = 28
    assert (T, NE, DK, FK, SLOT_HI) == (64, 8, 2, 2, 32)

    with ExitStack() as ctx:
        def sb(n, shape, dt=F32):
            return ctx.enter_context(nc.sbuf_tensor(f"{name}_{n}", shape, dt))

        def sem(n):
            return ctx.enter_context(nc.semaphore(f"{name}_{n}"))

        pair = [ctx.enter_context(nc.psum_tensor(f"{name}_pair{i}", [P, 2, 512], F32)) for i in range(2)]
        bank = [ctx.enter_context(nc.psum_tensor(f"{name}_bank{i}", [P, 512], F32)) for i in range(4)]
        ident = sb("ident", [P, P])
        ones = sb("ones", [P, P], BF16)
        before = sb("before", [P, P], BF16)
        count_i = sb("count_i", [P, T], I32)
        count_b = sb("count_b", [P, T], BF16)
        part_i = sb("part_i", [P, 1], I32)
        part = sb("part", [P, 1])
        gate_in = sb("gate_in", [NE, D])
        gateT = sb("gateT", [P, DK, NE])
        xin = [sb(f"xin{q}", [P, GT, D]) for q in range(2)]
        xn = [sb(f"xn{q}", [P, GT, D]) for q in range(2)]
        xnT = [sb(f"xnT{q}", [P, DK, GT * P]) for q in range(2)]
        stats = [sb(f"stats{q}", [P, GT, 6]) for q in range(2)]
        mv = [sb(f"mv{q}", [P, GT, 2]) for q in range(2)]
        var = [sb(f"var{q}", [P, GT]) for q in range(2)]
        std = [sb(f"std{q}", [P, GT]) for q in range(2)]
        rstd = [sb(f"rstd{q}", [P, GT]) for q in range(2)]
        prob = sb("prob", [P, NE, T])
        work = sb("work", [P, NE, T])
        first = sb("first", [P, NE, T])
        rank = sb("rank", [P, NE, T])
        csum = sb("csum", [P, NE, T])
        order = sb("order", [P, NE, T])
        score = sb("score", [P, T, NE])
        row_t = sb("row_t", [P, T])
        hit = sb("hit", [P, NE, T], BF16)
        count = sb("count", [P, NE], BF16)
        low = sb("low", [P, NE])
        cand = sb("cand", [P, NE])
        step = sb("step", [P, 1])
        got = sb("got", [P, NE])
        need = sb("need", [P, NE])
        onesT = sb("onesT", [P, T])
        through = sb("through", [P, NE, T])
        place = sb("place", [P, NE, T])
        keep = sb("keep", [P, NE, T])
        place_i = sb("place_i", [P, NE, T], I32)
        digit_i = sb("digit_i", [P, NE, T], I32)
        hi = sb("hi", [P, NE, T], BF16)
        lo = sb("lo", [P, NE, T], BF16)
        pick_hi = [sb(f"pick_hi{q}", [P, T, SLOT_HI], BF16) for q in range(2)]
        pick_lo = [sb(f"pick_lo{q}", [P, T, 2 * SLOT_LO], BF16) for q in range(2)]
        tile_of = sb("tile_of", [SLOT_HI, SLOT_LO])
        idx_hi = sb("idx_hi", [SLOT_HI, NE, SLOT_LO], I32)
        idx_all = sb("idx_all", [P, NE * J], I32)
        rows = [sb(f"rows{q}", [P, J, ROW]) for q in range(2)]
        w1_in = [sb(f"w1_in{q}", [P, FK, D]) for q in range(2)]
        w2_in = [sb(f"w2_in{q}", [P, DK, F]) for q in range(2)]
        w1T = [sb(f"w1T{q}", [P, DK, F]) for q in range(2)]
        w2T = [sb(f"w2T{q}", [P, FK, D]) for q in range(2)]
        xeT = sb("xeT", [P, DK, CAP])
        hT = sb("hT", [P, FK, CAP])
        slot_score = [sb(f"slot_score{q}", [P, J]) for q in range(2)]
        y = [sb(f"y{q}", [P, J, D]) for q in range(2)]

        residual_copied = sem("residual_copied")
        consts_ready = sem("consts_ready")
        pool_step = sem("pool_step")
        dve_step = sem("dve_step")
        gate_loaded = sem("gate_loaded")
        gateT_ps = sem("gateT_ps")
        gateT_ready = sem("gateT_ready")
        x_loaded = [sem(f"x_loaded{q}") for q in range(2)]
        var_ready = sem("var_ready")
        std_ready = sem("std_ready")
        xn_ready = sem("xn_ready")
        xn_stored = [sem(f"xn_stored{q}") for q in range(2)]
        xnT_ps = sem("xnT_ps")
        xnT_ready = sem("xnT_ready")
        logits_ps = sem("logits_ps")
        logits_ready = sem("logits_ready")
        shifted = sem("shifted")
        exped = sem("exped")
        score_ready = sem("score_ready")
        score_stored = sem("score_stored")
        count_ready = sem("count_ready")
        total_ps = sem("total_ps")
        mask_ready = sem("mask_ready")
        prefix_ps = sem("prefix_ps")
        picks_ready = sem("picks_ready")
        idx_ps = sem("idx_ps")
        idx_hi_ready = sem("idx_hi_ready")
        idx_moved = sem("idx_moved")
        w_loaded = [sem(f"w_loaded{q}") for q in range(2)]
        gathered = [sem(f"gathered{q}") for q in range(2)]
        turned_ps = sem("turned_ps")
        turned = sem("turned")
        h_ps = sem("h_ps")
        h_ready = sem("h_ready")
        y_ps = sem("y_ps")
        y_ready = sem("y_ready")
        slot_score_ready = sem("slot_score_ready")
        added = sem("added")

        src_g = src.rearrange("(g t p) d -> g p t d", t=GT, p=P)
        table_x = table[:, 0:D].rearrange("(g t p) d -> g p t d", t=GT, p=P)
        table_s = table[:, D:D + NE].rearrange("(t p) e -> p t e", p=P)
        w1_v = w1.rearrange("e (k p) d -> e p k d", p=P)
        w2_v = w2.rearrange("e (k p) f -> e p k f", p=P)
        idx_ps_bank = bank[3]

        def over_t(a):
            return a.unsqueeze(2).to_broadcast([P, NE, T])

        def over_e(a, n=NE):
            return a.unsqueeze(1).to_broadcast([P, n, T])

        with nc.Block() as block:

            @block.sync
            def _(sp):
                sp.dma_start(gate_in[:, :], gate_w).then_inc(gate_loaded, 16)
                for q in range(2):
                    sp.dma_start(xin[q][:, :, :], src_g[q]).then_inc(x_loaded[q], 16)
                if residual:
                    sp.dma_start(dst, src).then_inc(residual_copied, 16)

                def store_load(g, q, load):
                    sp.wait_ge(xn_ready, g + 1)
                    sp.dma_start(table_x[g], xn[q][:, :, :]).then_inc(xn_stored[q], 16)
                    if load:
                        sp.dma_start(xin[q][:, :, :], src_g[g + 2]).then_inc(x_loaded[q], 16)

                with sp.Fori(0, G // 2 - 1) as gp:
                    for q in range(2):
                        store_load(gp * 2 + q, q, True)
                for q in range(2):
                    store_load(G - 2 + q, q, False)
                    sp.dma_start(w1_in[q][:, :, :], w1_v[q]).then_inc(w_loaded[q], 16)
                    sp.dma_start(w2_in[q][:, :, :], w2_v[q]).then_inc(w_loaded[q], 16)
                sp.wait_ge(score_ready, 1)
                sp.dma_start(table_s, score[:, :, :]).then_inc(score_stored, 16)
                sp.wait_ge(idx_hi_ready, NE)
                for e in range(NE):
                    sp.dma_start(idx_all[:, e * J:(e + 1) * J],
                                 idx_hi[:, e, :].rearrange("a (c j) -> a c j", j=J)).then_inc(idx_moved, 16)
                with sp.Fori(0, NE // 2 - 1) as ep:
                    for q in range(2):
                        sp.wait_ge(turned_ps, (ep * 2 + q) * 3 + 1)
                        sp.dma_start(w1_in[q][:, :, :], w1_v[ep * 2 + q + 2]).then_inc(w_loaded[q], 16)
                        sp.dma_start(w2_in[q][:, :, :], w2_v[ep * 2 + q + 2]).then_inc(w_loaded[q], 16)

            @block.gpsimd
            def _(pool):
                ch = Chain(pool, pool_step)
                identity(pool, ch, ident[:, :])
                ch(pool.memset(before[:, :], 1.0))
                ch(pool.affine_select(out=before[:, :], in_=before[:, :], compare_op=ALU.is_gt, fill=0.0,
                                      base=0, pattern=[[1, P]], channel_multiplier=-1))
                pool.memset(ones[:, :], 1.0).then_inc(consts_ready, 1)
                ch(pool.iota(count_i[:, :], [[1, T]], base=0, channel_multiplier=0))
                ch(pool.iota(part_i[:, :], [[0, 1]], base=0, channel_multiplier=1))
                ch(pool.tensor_copy(count_b[:, :], count_i[:, :]))
                pool.tensor_copy(part[:, :], part_i[:, :]).then_inc(consts_ready, 1)

                def gather(e):
                    if e >= 2:
                        pool.wait_ge(turned_ps, (e - 1) * 3)
                        pool.wait_ge(slot_score_ready, e - 1)
                    for j in range(J):
                        pool.indirect_dma_start(
                            out=rows[e % 2][:, j, :], out_offset=None, in_=table,
                            in_offset=bass.IndirectOffsetOnAxis(ap=idx_all[:, e * J + j:e * J + j + 1], axis=0),
                        ).then_inc(gathered[e % 2], 16)

                def scatter(e):
                    if e >= 1:
                        pool.wait_ge(added, e * J * 16)
                    pool.wait_ge(y_ready, e * J + J)
                    for j in range(J):
                        pool.indirect_dma_start(
                            out=dst, out_offset=bass.IndirectOffsetOnAxis(ap=idx_all[:, e * J + j:e * J + j + 1], axis=0),
                            in_=y[e % 2][:, j, :], in_offset=None, compute_op=ALU.add,
                        ).then_inc(added, 16)

                pool.wait_ge(idx_moved, 16 * NE)
                pool.wait_ge(score_stored, 16)
                for q in range(2):
                    pool.wait_ge(xn_stored[q], 16 * (G // 2))
                if residual:
                    pool.wait_ge(residual_copied, 16)
                gather(0)
                for e in range(NE):
                    if e + 1 < NE:
                        gather(e + 1)
                    scatter(e)
                pool.wait_ge(added, NE * J * 16)

            @block.scalar
            def _(act):
                act.wait_ge(gateT_ps, 1)
                act.activation(gateT[:, :, :], bank[0][:, 0:DK * NE].rearrange("p (k e) -> p k e", k=DK),
                               ACT.Copy).then_inc(gateT_ready, 1)

                def normalise(gp, start):
                    for q in range(2):
                        g = gp * 2 + q
                        act.wait_ge(var_ready, g + 1)
                        act.activation(std[q][:, :], var[q][:, :], ACT.Sqrt).then_inc(std_ready, 1)
                    for q in range(2):
                        g = gp * 2 + q
                        act.wait_ge(xnT_ps, g + 1)
                        if not start:
                            act.wait_ge(logits_ps, g - 1)
                        act.activation(xnT[q][:, :, :], pair[q][:, :, :], ACT.Copy).then_inc(xnT_ready, 1)

                normalise(0, True)
                with act.Fori(1, G // 2) as gp:
                    normalise(gp, False)
                act.wait_ge(shifted, 1)
                act.activation(prob[:, :, :], work[:, :, :], ACT.Exp).then_inc(exped, 1)

                def expert(ep, q, start):
                    e = ep * 2 + q
                    ring = [pair[(3 * q + s) % 2] for s in range(3)]
                    act.wait_ge(turned_ps, e * 3 + 1)
                    if not start:
                        act.wait_ge(y_ps, e * J - J)
                    act.activation(w1T[q][:, :, :], ring[0][:, 0, :].rearrange("p (k f) -> p k f", k=DK), ACT.Copy)
                    act.activation(w2T[q][:, :, :], ring[0][:, 1, :].rearrange("p (k d) -> p k d", k=FK),
                                   ACT.Copy).then_inc(turned, 1)
                    for s in range(2):
                        act.wait_ge(turned_ps, e * 3 + 2 + s)
                        if s == 0 and (not start or q):
                            act.wait_ge(h_ps, e * 4)
                        act.activation(xeT[:, :, s * 512:(s + 1) * 512], ring[1 + s][:, :, :],
                                       ACT.Copy).then_inc(turned, 1)
                    if not start or q:
                        act.wait_ge(y_ps, e * J)
                    for s in range(2):
                        for f in range(FK):
                            n = 2 * s + f
                            act.wait_ge(h_ps, e * 4 + n + 1)
                            act.activation(hT[:, f, s * 512:(s + 1) * 512], bank[n % 2][:, :],
                                           ACT.Gelu).then_inc(h_ready, 1)

                for q in range(2):
                    expert(0, q, True)
                with act.Fori(1, NE // 2) as ep:
                    for q in range(2):
                        expert(ep, q, False)

            @block.vector
            def _(dve):
                ch = Chain(dve, dve_step)
                dve.wait_ge(consts_ready, 2)
                ch(dve.memset(onesT[:, :], 1.0))

                def statistics(gp):
                    for q in range(2):
                        dve.wait_ge(x_loaded[q], gp * 16 + 16)
                        for t in range(GT):
                            ch.add(dve.bn_stats(stats[q][:, t, :], xin[q][:, t, :]))
                        if q == 0:
                            ch.wait()
                    for q in range(2):
                        for t in range(GT):
                            ch.add(dve.bn_aggr(mv[q][:, t, :], stats[q][:, t, :]))
                        ch.wait()
                        dve.tensor_scalar(var[q][:, :], mv[q][:, :, 1], LN_EPS, None, ALU.add).then_inc(var_ready, 1)

                def scale(gp, q, start):
                    g = gp * 2 + q
                    dve.wait_ge(std_ready, g + 1)
                    ch(dve.reciprocal(rstd[q][:, :], std[q][:, :]))
                    if not start:
                        dve.wait_ge(xnT_ps, g - 1)
                        dve.wait_ge(xn_stored[q], gp * 16)
                    for t in range(GT):
                        last = dve.tensor_scalar(xn[q][:, t, :], xin[q][:, t, :], mv[q][:, t, 0:1],
                                                 rstd[q][:, t:t + 1], ALU.subtract, ALU.mult)
                    last.then_inc(xn_ready, 1)

                def take_logits(gp, q):
                    g = gp * 2 + q
                    dve.wait_ge(logits_ps, g + 1)
                    dve.tensor_copy(prob[:, :, bass.ds(g * GT, GT)],
                                    bank[q][:, 0:GT * NE].rearrange("p (t e) -> p e t", t=GT)).then_inc(logits_ready, 1)

                base = ch.n
                per = 2 * (2 * GT + 1)
                ch.at(base, 0, per)
                statistics(0)
                for q in range(2):
                    scale(0, q, True)
                with dve.Fori(1, G // 2) as gp:
                    ch.at(base, gp, per)
                    statistics(gp)
                    for q in range(2):
                        scale(gp, q, False)
                    for q in range(2):
                        take_logits(gp - 1, q)
                ch.after(base, G // 2, per)
                for q in range(2):
                    take_logits(G // 2 - 1, q)
                dve.wait_ge(logits_ready, G)

                def by_t(a):
                    return a[:, :, :].rearrange("p e t -> p t e")

                ch(dve.tensor_reduce(row_t[:, :], by_t(prob), AX.X, ALU.max))
                dve.tensor_tensor(work[:, :, :], prob[:, :, :], over_e(row_t[:, :]), ALU.subtract).then_inc(shifted, 1)
                dve.wait_ge(exped, 1)
                ch(dve.tensor_reduce(row_t[:, :], by_t(prob), AX.X, ALU.add))
                ch(dve.reciprocal(row_t[:, :], row_t[:, :]))
                ch(dve.tensor_tensor(prob[:, :, :], prob[:, :, :], over_e(row_t[:, :]), ALU.mult))

                ch(dve.memset(rank[:, :, :], 1.0))
                ch(dve.memset(csum[:, :, :], 0.0))
                for o in range(NE):
                    ch(dve.memset(first[:, o, :], 0.0))
                    if o > 0:
                        ch(dve.tensor_tensor(first[:, 0:o, :], over_e(prob[:, o, :], o), prob[:, 0:o, :], ALU.is_gt))
                    if o < NE - 1:
                        ch(dve.tensor_tensor(first[:, o + 1:, :], over_e(prob[:, o, :], NE - 1 - o),
                                             prob[:, o + 1:, :], ALU.is_ge))
                    ch(dve.tensor_tensor(rank[:, :, :], rank[:, :, :], first[:, :, :], ALU.add))
                    ch(dve.tensor_tensor(first[:, :, :], first[:, :, :], over_e(prob[:, o, :]), ALU.mult))
                    ch(dve.tensor_tensor(csum[:, :, :], csum[:, :, :], first[:, :, :], ALU.add))
                chosen = first
                ch(dve.tensor_scalar(chosen[:, :, :], csum[:, :, :], THRESHOLD, None, ALU.is_lt))
                ch(dve.tensor_tensor(work[:, :, :], prob[:, :, :], chosen[:, :, :], ALU.mult))
                dve.tensor_scalar(score[:, :, :], work[:, :, :].rearrange("p e t -> p t e"), 0.5, None,
                                  ALU.mult).then_inc(score_ready, 1)
                ch(dve.tensor_tensor(order[:, :, :], prob[:, :, :], rank[:, :, :], ALU.subtract))
                ch(dve.tensor_tensor(order[:, :, :], order[:, :, :], chosen[:, :, :], ALU.mult))
                ch(dve.tensor_scalar(work[:, :, :], chosen[:, :, :], -NOT_CHOSEN, NOT_CHOSEN, ALU.mult, ALU.add))
                ch(dve.tensor_tensor(order[:, :, :], order[:, :, :], work[:, :, :], ALU.add))

                def count_hits(threshold, op):
                    ch(dve.tensor_tensor(hit[:, :, :], order[:, :, :], over_t(threshold), op))
                    with nc.allow_low_precision("counts up to T are exact"):
                        dve.tensor_reduce(count[:, :], hit[:, :, :], AX.X, ALU.add).then_inc(count_ready, 1)

                ch(dve.memset(low[:, :], NOT_CHOSEN))
                ch(dve.memset(step[:, :], -NOT_CHOSEN / 2))
                start = ch.n + ch.base
                with dve.Fori(0, SEARCH) as s:
                    ch.at(start, s, 5)
                    ch(dve.tensor_scalar(cand[:, :], low[:, :], step[:, 0:1], None, ALU.add))
                    count_hits(cand[:, :], ALU.is_ge)
                    dve.wait_ge(total_ps, s + 1)
                    ch(dve.tensor_scalar(got[:, :], bank[2][:, 0:NE], float(CAP), step[:, 0:1], ALU.is_ge, ALU.mult))
                    ch(dve.tensor_tensor(low[:, :], low[:, :], got[:, :], ALU.add))
                    ch(dve.tensor_scalar(step[:, :], step[:, :], 0.5, None, ALU.mult))
                ch.after(start, SEARCH, 5)
                count_hits(low[:, :], ALU.is_gt)
                dve.wait_ge(total_ps, SEARCH + 1)
                ch(dve.tensor_scalar(need[:, :], bank[2][:, 0:NE], -1.0, float(CAP), ALU.mult, ALU.add))
                ch(dve.tensor_copy(keep[:, :, :], hit[:, :, :]))
                dve.tensor_tensor(hit[:, :, :], order[:, :, :], over_t(low[:, :]), ALU.is_equal).then_inc(mask_ready, 1)

                def places(n):
                    dve.wait_ge(prefix_ps, n)
                    tiles = bank[3][:, :].rearrange("p (e t) -> p e t", e=NE)
                    for e in range(NE):
                        ch(dve.tensor_tensor_scan(through[:, e, :], onesT[:, :], tiles[:, e, :], 0.0, ALU.mult, ALU.add))
                    ch(dve.tensor_tensor(through[:, :, :], through[:, :, :], tiles, ALU.subtract))
                    ch(dve.tensor_tensor(place[:, :, :], through[:, :, :],
                                         bank[2][:, :].rearrange("p (e t) -> p e t", e=NE), ALU.add))

                dve.wait_ge(mask_ready, 1)
                places(1)
                ch(dve.tensor_tensor(work[:, :, :], place[:, :, :], over_t(need[:, :]), ALU.is_lt))
                ch(dve.tensor_tensor(work[:, :, :], work[:, :, :], hit[:, :, :], ALU.mult))
                ch(dve.tensor_tensor(keep[:, :, :], keep[:, :, :], work[:, :, :], ALU.add))
                dve.tensor_copy(hit[:, :, :], keep[:, :, :]).then_inc(mask_ready, 1)
                places(2)
                ch(dve.tensor_copy(place_i[:, :, :], place[:, :, :]))
                ch(dve.tensor_scalar(digit_i[:, :, :], place_i[:, :, :], SLOT_LO - 1, None, ALU.bitwise_and))
                ch(dve.tensor_copy(lo[:, :, :], digit_i[:, :, :]))
                ch(dve.tensor_scalar(digit_i[:, :, :], place_i[:, :, :], SLOT_LO.bit_length() - 1, None,
                                     ALU.logical_shift_right))
                ch(dve.tensor_copy(work[:, :, :], digit_i[:, :, :]))
                ch(dve.tensor_scalar(work[:, :, :], work[:, :, :], 1.0, None, ALU.add))
                ch(dve.tensor_tensor(work[:, :, :], work[:, :, :], keep[:, :, :], ALU.mult))
                ch(dve.tensor_scalar(hi[:, :, :], work[:, :, :], -1.0, None, ALU.add))

                shape = [P, T, SLOT_LO]
                digits = count_b[:, 0:SLOT_LO].unsqueeze(1).to_broadcast(shape)

                def take_idx(ep, q):
                    e = ep * 2 + q
                    dve.wait_ge(idx_ps, e + 1)
                    ch(dve.tensor_copy(tile_of[:, :], idx_ps_bank[0:SLOT_HI, SLOT_LO:2 * SLOT_LO]))
                    dve.scalar_tensor_tensor(
                        out=idx_hi[:, bass.ds(e, 1), :].rearrange("a e l -> a (e l)"),
                        in0=tile_of[:, :], scalar=float(P),
                        in1=idx_ps_bank[0:SLOT_HI, 0:SLOT_LO], op0=ALU.mult, op1=ALU.add).then_inc(idx_hi_ready, 1)

                def picks(ep, q, start):
                    e = ep * 2 + q
                    if not start:
                        dve.wait_ge(idx_ps, e - 1)

                    def of(a):
                        return a[:, bass.ds(e, 1), :].rearrange("p e t -> p (e t)").unsqueeze(2).to_broadcast(shape)

                    dve.tensor_tensor(pick_hi[q][:, :, :], digits, of(hi), ALU.is_equal).then_inc(picks_ready, 1)
                    ch(dve.tensor_tensor(pick_lo[q][:, :, 0:SLOT_LO], digits, of(lo), ALU.is_equal))
                    ch(dve.tensor_tensor(pick_lo[q][:, :, SLOT_LO:], pick_lo[q][:, :, 0:SLOT_LO],
                                         count_b[:, :].unsqueeze(2).to_broadcast(shape), ALU.mult))
                    dve.tensor_scalar(pick_lo[q][:, :, 0:SLOT_LO], pick_lo[q][:, :, 0:SLOT_LO], part[:, 0:1], None,
                                      ALU.mult).then_inc(picks_ready, 1)

                picks(0, 0, True)
                picks(0, 1, True)
                take_idx(0, 0)
                start = ch.base + ch.n - 6
                with dve.Fori(1, NE // 2) as ep:
                    ch.at(start, ep, 6)
                    picks(ep, 0, False)
                    take_idx(ep - 1, 1)
                    picks(ep, 1, False)
                    take_idx(ep, 0)
                ch.after(start, NE // 2, 6)
                take_idx(NE // 2 - 1, 1)

                def expert(ep, q, start):
                    e = ep * 2 + q
                    dve.wait_ge(gathered[q], ep * (16 * J) + 16 * J)
                    if not start:
                        dve.wait_ge(added, e * (J * 16) - J * 16)
                    dve.tensor_copy(slot_score[q][:, :], rows[q][:, :, bass.ds(e + D, 1)].rearrange("p j e -> p (j e)")
                                    ).then_inc(slot_score_ready, 1)
                    dve.wait_ge(slot_score_ready, e + 1)
                    for j in range(J):
                        dve.wait_ge(y_ps, e * J + j + 1)
                        dve.tensor_scalar(y[q][:, j, :], bank[2 + j % 2][:, 0:D],
                                          slot_score[q][:, j:j + 1], None, ALU.mult).then_inc(y_ready, 1)

                for q in range(2):
                    expert(0, q, True)
                with dve.Fori(1, NE // 2) as ep:
                    for q in range(2):
                        expert(ep, q, False)

            @block.tensor
            def _(pe):
                pe.wait_ge(consts_ready, 2)
                pe.wait_ge(gate_loaded, 16)
                for k in range(DK):
                    last = pe.transpose(bank[0][:, k * NE:(k + 1) * NE], gate_in[:, k * P:(k + 1) * P], ident[0:NE, 0:NE])
                last.then_inc(gateT_ps, 1)
                pe.wait_ge(gateT_ready, 1)

                def normalise(gp, start):
                    for q in range(2):
                        g = gp * 2 + q
                        pe.wait_ge(xn_ready, g + 1)
                        if not start:
                            pe.wait_ge(xnT_ready, g - 1)
                        for t in range(GT):
                            for k in range(DK):
                                last = pe.transpose(pair[q][:, k, t * P:(t + 1) * P], xn[q][:, t, k * P:(k + 1) * P],
                                                    ident[:, :])
                        last.then_inc(xnT_ps, 1)
                    for q in range(2):
                        g = gp * 2 + q
                        pe.wait_ge(xnT_ready, g + 1)
                        if not start:
                            pe.wait_ge(logits_ready, g - 1)
                        for t in range(GT):
                            for k in range(DK):
                                last = pe.matmul(bank[q][:, t * NE:(t + 1) * NE], xnT[q][:, k, t * P:(t + 1) * P],
                                                 gateT[:, k, :], start=(k == 0), stop=(k == DK - 1))
                        last.then_inc(logits_ps, 1)

                normalise(0, True)
                with pe.Fori(1, G // 2) as gp:
                    normalise(gp, False)

                with pe.Fori(0, SEARCH + 1) as s:
                    pe.wait_ge(count_ready, s + 1)
                    pe.matmul(bank[2][:, 0:NE], ones[:, :], count[:, :], start=True, stop=True).then_inc(total_ps, 1)
                for n in range(2):
                    pe.wait_ge(mask_ready, n + 1)
                    mask = hit[:, :, :].rearrange("p e t -> p (e t)")
                    pe.matmul(bank[2][:, :], before[:, :], mask, start=True, stop=True)
                    pe.matmul(bank[3][:, :], ones[:, :], mask, start=True, stop=True).then_inc(prefix_ps, 1)

                def slots(ep, q, start):
                    e = ep * 2 + q
                    pe.wait_ge(picks_ready, e * 2 + 2)
                    if not start or q:
                        pe.wait_ge(idx_hi_ready, e)
                    for t in range(T):
                        last = pe.matmul(idx_ps_bank[0:SLOT_HI, 0:2 * SLOT_LO], pick_hi[q][:, t, :], pick_lo[q][:, t, :],
                                         start=(t == 0), stop=(t == T - 1))
                    last.then_inc(idx_ps, 1)

                for q in range(2):
                    slots(0, q, True)
                with pe.Fori(1, NE // 2) as ep:
                    for q in range(2):
                        slots(ep, q, False)

                def expert(ep, q, start):
                    e = ep * 2 + q
                    ring = [pair[(3 * q + s) % 2] for s in range(3)]

                    def free(s):
                        if not start or 3 * q + s >= 2:
                            pe.wait_ge(turned, e * 3 + s - 1)

                    pe.wait_ge(w_loaded[q], ep * 32 + 32)
                    free(0)
                    for k in range(DK):
                        for f in range(FK):
                            pe.transpose(ring[0][:, 0, (k * FK + f) * P:(k * FK + f + 1) * P],
                                         w1_in[q][:, f, k * P:(k + 1) * P], ident[:, :])
                    for f in range(FK):
                        for k in range(DK):
                            last = pe.transpose(ring[0][:, 1, (f * DK + k) * P:(f * DK + k + 1) * P],
                                                w2_in[q][:, k, f * P:(f + 1) * P], ident[:, :])
                    last.then_inc(turned_ps, 1)
                    pe.wait_ge(gathered[q], ep * (16 * J) + 16 * J)
                    for s in range(2):
                        free(1 + s)
                        for t in range(J // 2):
                            for k in range(DK):
                                last = pe.transpose(ring[1 + s][:, k, t * P:(t + 1) * P],
                                                    rows[q][:, s * (J // 2) + t, k * P:(k + 1) * P], ident[:, :])
                        last.then_inc(turned_ps, 1)
                    for s in range(2):
                        pe.wait_ge(turned, e * 3 + 2 + s)
                        for f in range(FK):
                            n = 2 * s + f
                            if not start or q or n >= 2:
                                pe.wait_ge(h_ready, e * 4 + n - 1)
                            for k in range(DK):
                                last = pe.matmul(bank[n % 2][:, :], w1T[q][:, k, f * P:(f + 1) * P],
                                                 xeT[:, k, s * 512:(s + 1) * 512], start=(k == 0), stop=(k == DK - 1))
                            last.then_inc(h_ps, 1)
                    for j in range(J):
                        pe.wait_ge(h_ready, e * 4 + (2 if j < J // 2 else 4))
                        if not start or q or j >= 2:
                            pe.wait_ge(y_ready, e * J + j - 1)
                        for f in range(FK):
                            last = pe.matmul(bank[2 + j % 2][:, 0:D], hT[:, f, j * P:(j + 1) * P],
                                             w2T[q][:, f, :], start=(f == 0), stop=(f == FK - 1))
                        last.then_inc(y_ps, 1)

                for q in range(2):
                    expert(0, q, True)
                with pe.Fori(1, NE // 2) as ep:
                    for q in range(2):
                        expert(ep, q, False)


def build_attention(nc, x, Wq, Wk, Wv, Wr, Wo, q_parts, k_parts, B):
    N = x.shape[0]
    S = N // B
    TB = S // P
    T = N // P
    H, K = 16, Wr.shape[1] // 16
    HD = D // H
    NF = HD // 2
    HK = H * K
    VW = HD + 1
    EPS = 1e-8
    HALF_SCALE = HD ** -0.25
    LIMIT = 40.0
    MAX_POS = 2048 - 1
    ROPE_BASE = 10000.0
    PARTS = 3
    KQ = 6 * HD
    KS = KQ + 2
    Q_ROWS = [(0, 3, 0), (3, 2, 0), (5, 1, 0)]
    K_ROWS = [(0, 3, 0), (3, 2, 1), (5, 1, 2)]
    CH = 4
    NC = TB // CH
    HEADS = B * H
    LEAD = TB + 2
    NEG = -1e30
    ROUND = 1.5 * 2.0 ** 23
    PI = float(np.pi)
    TWO_PI_HI = 6.28125
    TWO_PI_LO = 2.0 * PI - TWO_PI_HI
    freq = [float(f) for f in np.float32(1.0) / np.float32(ROPE_BASE) ** (np.arange(0, HD, 2, dtype=np.float32) / HD)]
    assert (TB, H, K, NC, HEADS) == (16, 16, 4, 4, T)

    units = []
    for c in range(NC):
        units += [(c, 2 * p, 0) for p in range(2 * c)] + [(c, CH * c, 0), (c, CH * c + 2, 2)]
    NU = len(units)
    last_of = [max(u for u in range(NU) if units[u][0] == c) for c in range(NC)]
    pieces = [(t, a, min(1024, (t + 1) * P - a)) for t in range(TB) for a in range(0, (t + 1) * P, 1024)]
    NP = len(pieces)

    with ExitStack() as ctx:
        def sb(n, shape, dt=F32):
            return ctx.enter_context(nc.sbuf_tensor(f"at_{n}", shape, dt))

        def sem(n):
            return ctx.enter_context(nc.semaphore(f"at_{n}"))

        ring = [ctx.enter_context(nc.psum_tensor(f"at_ring{i}", [P, 2, 512], F32)) for i in range(2)]
        mix = [ctx.enter_context(nc.psum_tensor(f"at_mix{i}", [P, 512], F32)) for i in range(2)]
        side = [ctx.enter_context(nc.psum_tensor(f"at_side{i}", [P, 512], F32)) for i in range(2)]

        ident = sb("ident", [P, P])
        ident_b = sb("ident_b", [P, P], BF16)
        ones = sb("ones", [P, P])
        before = sb("before", [P, P])
        late_kq = sb("late_kq", [P, P], BF16)
        late_qk = sb("late_qk", [P, P], BF16)
        sq_max = sb("sq_max", [P, 1])
        sq_top = sb("sq_top", [1, 1])
        sq_tile = sb("sq_tile", [P, 1])
        sq_head = sb("sq_head", [P, 2 * H])
        bounded = sb("bounded", [1, T], I32)
        freq_t = sb("freq_t", [P, NF, HK])
        cos1 = sb("cos1", [P, 1, NF * H])
        sin1 = sb("sin1", [P, 1, NF * H])
        half_pi = sb("half_pi", [P, 1])
        eps_t = sb("eps_t", [P, 1])
        carry_i = sb("carry_i", [P, T + 1], I32)
        carry = sb("carry", [P, T + 1])
        w_all = sb("w_all", [P, DK, 3 * D + HK])
        wo = sb("wo", [P, DK, D])
        vo = sb("vo", [P, T, D])
        prob = sb("prob", [P, T, HK])
        xin = sb("xin", [P, D])
        stats = sb("stats", [P, 6])
        mv = sb("mv", [P, 2])
        var = sb("var", [P, 1])
        logv = sb("logv", [P, 1])
        rs0 = sb("rs0", [P, 1])
        rs1 = sb("rs1", [P, 1])
        xn = sb("xn", [P, D])
        turned = sb("turned", [P, 4, P])
        qk = sb("qk", [P, 2 * D])
        logit = sb("logit", [P, HK])
        small = sb("small", [P, H])
        lexp = sb("lexp", [P, HK])
        p_t = sb("p_t", [P, HK])
        acc = sb("acc", [P, HK])
        pos = sb("pos", [P, HK])
        pos_i = sb("pos_i", [P, HK], I32)
        base_t = sb("base_t", [P, HK])
        over_t = sb("over_t", [P, HK])
        g_t = sb("g_t", [P, HK])
        theta = sb("theta", [P, NF, HK])
        whole = sb("whole", [P, NF * HK])
        angle = sb("angle", [P, NF * HK])
        angle_abs = sb("angle_abs", [P, NF * HK])
        cs = sb("cs", [P, 2, NF * HK])
        prods = sb("prods", [P, 4, NF * HK])
        sums = sb("sums", [P, 4, NF * H])
        cs_a = sb("cs_a", [P, 2, NF * H])
        cs_b = sb("cs_b", [P, 2, NF * H])
        cosw = sb("cosw", [P, NF * H])
        sinw = sb("sinw", [P, NF * H])
        nsinw = sb("nsinw", [P, NF * H])
        rot_a = sb("rot_a", [P, 2 * D])
        rot_b = sb("rot_b", [P, 2 * D])
        qkr = sb("qkr", [P, 2 * D])
        rest = sb("rest", [P, 4, P])
        parts = sb("parts", [P, 4, PARTS, P], BF16)
        qT = [sb(f"qT{q}", [KS, S], BF16) for q in range(2)]
        kT = [sb(f"kT{q}", [KS, S], BF16) for q in range(2)]
        val = [sb(f"val{q}", [P, TB, K, VW]) for q in range(2)]
        NE_BUF = 4
        ew = [sb(f"ew{n}", [P, 2, 512]) for n in range(NE_BUF)]
        mixed = sb("mixed", [P, CH, K, VW])
        summed = sb("summed", [P, CH, VW])
        recip = sb("recip", [P, CH])
        top = sb("top", [P, NP])
        ntop = sb("ntop", [P, TB])
        shift = sb("shift", [TB, 2, P], BF16)
        ostage = sb("ostage", [P, D])
        xres = sb("xres", [P, D])
        yout = sb("yout", [P, D])

        names = ("consts_ready pool_step dve_step act_step w_loaded w_scaled x_loaded var_ready rs_ready xn_ready xnT_ps "
                 "oT_ps turned_ready qkv_ps qk_copied vr_copied lg_shifted p_exped p_ready p_saved pos_ps pos_taken "
                 "pf_ready theta_ready angle_ready trig_abs trig_ready g_ready gprod_ready roped qkT_ps rest_ready mid_ready "
                 "lo_ready part_stored s_ps exp_ready av_done u_taken val_ready o_ready max_ps max_taken "
                 "top_ready topT_ps shift_ready shift_loaded sq_ready sq_max_ready bounded_ready max_step o_staged res_loaded post_ps post_summed out_stored").split()
        s = {n: sem(n) for n in names}
        qk_loaded = [sem(f"qk_loaded{q}") for q in range(2)]

        x_v = x.rearrange("(t p) d -> t p d", p=P)
        q_tile = q_parts.rearrange("(b g h) d a s -> b g (h d) a s", b=B, g=2)
        k_tile = k_parts.rearrange("(b g h) d a s -> b g (h d) a s", b=B, g=2)

        def of_head(a, i, w):
            v = a[:, :, :].rearrange("p (b t) (h d) -> p b t h d", b=B, h=H)
            return v[:, bass.ds(i // H, 1), :, bass.ds(i % H, 1), :].rearrange("p b t h d -> p (b t) (h d)")

        def row(a, t):
            return a[:, bass.ds(t, 1), :].rearrange("p t d -> p (t d)")

        PRIME_S, PRIME_U, PRIME_M, PRIME_E = 2, 2, 2, NU + NE_BUF

        def scores_bounded(eng, fin):
            tile = fin - 1 if fin is not None else T - 1
            return eng.value_load(bounded[0:1, bass.ds(tile, 1)], min_val=0, max_val=1)

        def schedule(eng, run, first_head=None):
            run(0, 0, new=0)
            with eng.Fori(1, LEAD) as t:
                run(0, 0, new=t, fin=t - 1)
            if first_head is not None:
                first_head()
            with eng.Fori(0, LEAD // 2) as ip:
                for q in range(2):
                    i = ip * 2 + q
                    run(ip, q, new=i + LEAD, fin=i + LEAD - 1, head=i)
            with eng.Fori(LEAD // 2, (HEADS - LEAD) // 2 - 1) as ip:
                for q in range(2):
                    i = ip * 2 + q
                    run(ip, q, new=i + LEAD, fin=i + LEAD - 1, head=i, post=i - LEAD)
            for i in range(HEADS - LEAD - 2, HEADS - LEAD + 2):
                run(i // 2, i % 2, new=i + LEAD if i + LEAD < T else None,
                    fin=i + LEAD - 1 if i + LEAD - 1 < T else None, head=i, post=i - LEAD)
            with eng.Fori((HEADS - LEAD) // 2 + 1, HEADS // 2 - 1) as ip:
                for q in range(2):
                    i = ip * 2 + q
                    run(ip, q, head=i, post=i - LEAD)
            for i in (HEADS - 2, HEADS - 1):
                run(i // 2, i % 2, head=i, post=i - LEAD)
            with eng.Fori(HEADS - LEAD, T) as t:
                run(0, 0, post=t)

        def is_last(i, count):
            return isinstance(i, int) and i == count - 1

        with nc.Block() as block:

            @block.sync
            def _(sp):
                sp.sem_inc(s["part_stored"], 64)
                sp.sem_inc(s["shift_loaded"], 32)
                sp.sem_inc(s["out_stored"], 16)
                for n, (w, o) in enumerate(((Wq, 0), (Wk, D), (Wv, 2 * D), (Wr, 3 * D))):
                    sp.dma_start(w_all[:, :, o:o + w.shape[1]], w.rearrange("(k p) n -> p k n", p=P)).then_inc(s["w_loaded"], 16)
                sp.dma_start(wo[:, :, :], Wo.rearrange("(k p) n -> p k n", p=P)).then_inc(s["w_loaded"], 16)
                sp.dma_start(xin[:, :], x_v[0]).then_inc(s["x_loaded"], 16)

                def load_head(j, q, tiles):
                    if not (isinstance(j, int) and j == 0):
                        sp.wait_ge(s["av_done"], (j - 1) * NU + PRIME_E)
                    sp.wait_ge(s["part_stored"], tiles * 64 + 64)
                    for (dst, src, rows) in ((qT, q_parts, Q_ROWS), (kT, k_parts, K_ROWS)):
                        head = src[bass.ds(j, 1)].rearrange("h d a s -> (h d) a s")
                        for at, n, first in rows:
                            if src is q_parts:
                                part = head[:, first:first + n, :].rearrange("d a s -> a d s")
                            else:
                                part = head[:, first, :].unsqueeze(0).to_broadcast([n, HD, S])
                            sp.dma_start(dst[q][at * HD:(at + n) * HD, :], part).then_inc(qk_loaded[q], 16)

                def load_shift(j, q, fin):
                    with sp.If(scores_bounded(sp, fin) < 1):
                        sp.wait_ge(s["shift_ready"], j + 1)
                        for r in range(2):
                            sp.dma_start(qT[q][KQ + r:KQ + r + 1, :], shift[:, r, :]).then_inc(s["shift_loaded"], 16)
                    with sp.Else():
                        sp.sem_inc(s["shift_loaded"], 32)

                def first_head():
                    load_head(0, 0, TB)
                    load_shift(0, 0, TB)

                def run(ip, q, new=None, fin=None, head=None, post=None):
                    if new is not None and not is_last(new, T):
                        sp.wait_ge(s["xn_ready"], new + 1)
                        sp.dma_start(xin[:, :], x_v[new + 1]).then_inc(s["x_loaded"], 16)
                    if head is not None and not is_last(head, HEADS):
                        load_head(head + 1, 1 - q, head + 1 + TB if fin is not None else T)
                    if post is not None:
                        sp.wait_ge(s["post_summed"], post + 1)
                        sp.dma_start(xres[:, :], x_v[post]).then_inc(s["res_loaded"], 16)
                    if fin is not None:
                        sp.wait_ge(s["lo_ready"], fin + 1)
                        for n in range(4):
                            dst = (q_tile, k_tile)[n // 2][fin // TB, n % 2][:, :, bass.ds((fin % TB) * P, P)]
                            sp.dma_start(dst, parts[:, n, :, :]).then_inc(s["part_stored"], 16)
                    if head is not None and not is_last(head, HEADS):
                        load_shift(head + 1, 1 - q, fin)
                    if post is not None:
                        sp.wait_ge(s["post_summed"], post + 2)
                        sp.dma_start(x_v[post], yout[:, :]).then_inc(s["out_stored"], 16)

                schedule(sp, run, first_head)
                sp.wait_ge(s["out_stored"], T * 16 + 16)

            @block.gpsimd
            def _(pool):
                ch = Chain(pool, s["pool_step"])
                identity(pool, ch, ident[:, :])
                ch(pool.tensor_copy(ident_b[:, :], ident[:, :]))
                ch(pool.memset(before[:, :], 1.0))
                ch(pool.affine_select(out=before[:, :], in_=before[:, :], compare_op=ALU.is_gt, fill=0.0,
                                      base=0, pattern=[[1, P]], channel_multiplier=-1))
                for m, a in ((late_kq, 1), (late_qk, -1)):
                    ch(pool.memset(m[:, :], 0.0))
                    ch(pool.affine_select(out=m[:, :], in_=m[:, :], compare_op=ALU.is_ge, fill=NEG,
                                          base=0, pattern=[[a, P]], channel_multiplier=-a))
                ch(pool.memset(ones[:, :], 1.0))
                for f in range(NF):
                    ch(pool.memset(freq_t[:, f, :], freq[f]))
                    ch(pool.memset(cos1[:, :, f * H:(f + 1) * H], float(np.cos(freq[f]) - 1.0)))
                    ch(pool.memset(sin1[:, :, f * H:(f + 1) * H], float(np.sin(freq[f]))))
                ch(pool.memset(half_pi[:, :], PI / 2))
                ch(pool.memset(eps_t[:, :], EPS))
                for q in range(2):
                    ch(pool.memset(qT[q][KQ:KS, :], 0.0))
                    ch(pool.memset(kT[q][KQ:KS, :], 1.0))
                ch(pool.iota(carry_i[:, 0:T], [[0, B], [1, TB]], base=0, channel_multiplier=0))
                ch(pool.memset(carry_i[:, T:T + 1], 0.0))
                ch(pool.tensor_copy(carry[:, :], carry_i[:, :]))
                pool.tensor_scalar(carry[:, :], carry[:, :], 1.0, None, ALU.min).then_inc(s["consts_ready"], 1)

                def weigh_values(j, q, tiles):
                    pool.wait_ge(s["av_done"], (j - 1) * NU + PRIME_E)
                    pool.wait_ge(s["p_saved"], tiles)
                    vv, pp = of_head(vo, j, HD), of_head(prob, j, K)
                    pool.tensor_tensor(val[q][:, :, :, HD], pp, eps_t[:, :].unsqueeze(2).to_broadcast([P, TB, K]),
                                       ALU.add).then_inc(s["val_ready"], 1)
                    pool.wait_ge(s["val_ready"], j * 2 + 1)
                    pool.tensor_tensor(val[q][:, :, :, 0:HD], vv.unsqueeze(2).to_broadcast([P, TB, K, HD]),
                                       val[q][:, :, :, HD].unsqueeze(3).to_broadcast([P, TB, K, HD]),
                                       ALU.mult).then_inc(s["val_ready"], 1)

                def run(ip, q, new=None, fin=None, head=None, post=None):
                    if post is not None:
                        pool.wait_ge(s["o_ready"], (post + TB) * NC if head is not None else HEADS * NC)
                        pool.wait_ge(s["post_summed"], post + 1)
                        pool.tensor_copy(ostage[:, :], row(vo, post)).then_inc(s["o_staged"], 1)
                    if head is not None and not is_last(head, HEADS):
                        weigh_values(head + 1, 1 - q, head + 1 + TB if fin is not None else T)
                    if fin is not None:
                        pool.wait_ge(s["trig_ready"], fin + 1)
                        pool.wait_ge(s["g_ready"], fin + 1)
                        pool.tensor_tensor(
                            prods[:, 2:4, :].rearrange("p c (f n) -> p (c f) n", n=HK),
                            cs[:, :, :].rearrange("p c (f n) -> p (c f) n", n=HK),
                            g_t[:, :].unsqueeze(1).to_broadcast([P, 2 * NF, HK]), ALU.mult).then_inc(s["gprod_ready"], 1)
                        pool.wait_ge(s["roped"], fin + 1)
                        pool.tensor_tensor(rot_a[:, :], qkr[:, :], qkr[:, :], ALU.mult).then_inc(s["sq_ready"], 1)
                    if new is not None:
                        pool.wait_ge(s["p_ready"], new + 1)
                        pool.tensor_copy(row(prob, new), p_t[:, :]).then_inc(s["p_saved"], 1)
                        pool.wait_ge(s["pf_ready"], new + 1)
                        pool.tensor_tensor(theta[:, :, :], freq_t[:, :, :], base_t[:, :].unsqueeze(1).to_broadcast([P, NF, HK]),
                                           ALU.mult).then_inc(s["theta_ready"], 1)
                    if fin is not None:
                        pool.wait_ge(s["mid_ready"], fin + 1)
                        pool.tensor_tensor(parts[:, :, 2, :], rest[:, :, :], parts[:, :, 1, :], ALU.subtract).then_inc(s["lo_ready"], 1)

                schedule(pool, run, lambda: weigh_values(0, 0, TB))

            @block.scalar
            def _(act):
                act.wait_ge(s["w_loaded"], 16 * 5)
                act.wait_ge(s["consts_ready"], 1)
                act.sem_inc(s["exp_ready"], PRIME_S)
                act.activation(w_all[:, :, 0:2 * D], w_all[:, :, 0:2 * D], ACT.Copy, scale=HALF_SCALE).then_inc(s["w_scaled"], 1)
                act.preload_act_table_set("natural_log_exp_and_others")

                def rsqrt(t):
                    act.wait_ge(s["var_ready"], t + 1)
                    act.activation(logv[:, :], var[:, :], ACT.Ln).then_inc(s["act_step"], 1)
                    act.wait_ge(s["act_step"], t + 1)
                    act.activation(rs0[:, :], logv[:, :], ACT.Exp, scale=-0.5).then_inc(s["rs_ready"], 1)

                def weights(i, u):
                    c, j, t0 = units[u]
                    w = 512 - t0 * P
                    act.wait_ge(s["s_ps"], i * NU + u + 1)
                    act.wait_ge(s["av_done"], i * NU + u + 1 + NU)
                    out, src = ew[u % NE_BUF], ring[u % 2]
                    if t0 == 0:
                        act.activation(out[:, :, :], src[:, :, :], ACT.Exp).then_inc(s["exp_ready"], 1)
                    else:
                        act.activation(out[:, 0, :], src[:, 0, :], ACT.Exp).then_inc(s["exp_ready"], 1)

                rsqrt(0)

                def run(ip, q, new=None, fin=None, head=None, post=None):
                    start = isinstance(new, int) and new == 0

                    def trig():
                        if fin is None:
                            return
                        act.wait_ge(s["angle_ready"], fin + 1)
                        if not (isinstance(fin, int) and fin == 0):
                            act.wait_ge(s["roped"], fin)
                            act.wait_ge(s["gprod_ready"], fin)
                        act.activation(angle_abs[:, :], angle[:, :], ACT.Abs).then_inc(s["trig_abs"], 1)
                        act.activation(cs[:, 1, :], angle[:, :], ACT.Sin)
                        act.wait_ge(s["trig_abs"], fin + 1)
                        act.activation(cs[:, 0, :], angle_abs[:, :], ACT.Sin, bias=half_pi[:, 0:1], scale=-1.0).then_inc(s["trig_ready"], 1)
                        act.preload_act_table_set("natural_log_exp_and_others")

                    def copy_turned():
                        if new is None and post is None:
                            return
                        a, b = (0 if new is not None else 2), (4 if post is not None else 2)
                        if new is not None:
                            act.wait_ge(s["xnT_ps"], new + 1)
                            if not start:
                                act.wait_ge(s["qkv_ps"], new)
                        if post is not None:
                            act.wait_ge(s["oT_ps"], post + 1)
                            act.wait_ge(s["post_summed"], post + 1)
                        act.activation(turned[:, a:b, :], side[0][:, a * P:b * P].rearrange("p (n c) -> p n c", c=P),
                                       ACT.Copy).then_inc(s["turned_ready"], 1)

                    def copy_qkv():
                        if new is None:
                            return
                        act.wait_ge(s["qkv_ps"], new + 1)
                        if not start:
                            act.wait_ge(s["roped"], new)
                        act.activation(qk[:, :], side[1][:, :], ACT.Copy).then_inc(s["qk_copied"], 1)
                        if not start:
                            act.wait_ge(s["p_ready"], new)
                        act.activation(row(vo, new), side[0][:, 0:D], ACT.Copy).then_inc(s["vr_copied"], 1)
                        act.activation(logit[:, :], side[0][:, D:D + HK], ACT.Copy).then_inc(s["vr_copied"], 1)

                    def softmax_exp():
                        if new is None:
                            return
                        act.wait_ge(s["lg_shifted"], new + 1)
                        act.activation(lexp[:, :], logit[:, :], ACT.Exp).then_inc(s["p_exped"], 1)

                    def next_rsqrt():
                        if new is not None and not is_last(new, T):
                            rsqrt(new + 1)

                    def middle_part():
                        if fin is None:
                            return
                        act.wait_ge(s["rest_ready"], fin + 1)
                        act.activation(parts[:, :, 1, :], rest[:, :, :], ACT.Copy).then_inc(s["mid_ready"], 1)

                    side_steps = {1: trig, 5: copy_turned, 9: copy_qkv, 12: softmax_exp, 14: next_rsqrt, 18: middle_part}
                    for u in range(NU):
                        if u in side_steps:
                            side_steps[u]()
                        if head is not None:
                            weights(head, u)

                schedule(act, run)

            @block.vector
            def _(dve):
                ch = Chain(dve, s["dve_step"])
                dve.sem_inc(s["u_taken"], PRIME_U)
                dve.sem_inc(s["max_taken"], PRIME_M)
                dve.sem_inc(s["post_summed"], 1)
                dve.wait_ge(s["consts_ready"], 1)
                dve.sem_inc(s["bounded_ready"], 1)
                ch(dve.memset(acc[:, :], 0.0))
                ch(dve.memset(sq_max[:, :], 0.0))

                def gather_statistics(t):
                    dve.wait_ge(s["x_loaded"], t * 16 + 16)
                    ch.add(dve.bn_stats(stats[:, :], xin[:, :]))

                def statistics(t):
                    ch(dve.bn_aggr(mv[:, :], stats[:, :]))
                    dve.tensor_scalar(var[:, :], mv[:, 1:2], LN_EPS, None, ALU.add).then_inc(s["var_ready"], 1)

                def normalise(t, first=False):
                    dve.wait_ge(s["rs_ready"], t + 1)
                    ch(dve.tensor_tensor(rs1[:, :], rs0[:, :], rs0[:, :], ALU.mult))
                    ch(dve.tensor_tensor(rs1[:, :], rs1[:, :], var[:, :], ALU.mult))
                    ch(dve.tensor_scalar(rs1[:, :], rs1[:, :], -0.5, 1.5, ALU.mult, ALU.add))
                    ch(dve.tensor_tensor(rs1[:, :], rs1[:, :], rs0[:, :], ALU.mult))
                    if not first:
                        dve.wait_ge(s["xnT_ps"], t)
                    dve.tensor_scalar(xn[:, :], xin[:, :], mv[:, 0:1], rs1[:, 0:1], ALU.subtract, ALU.mult).then_inc(s["xn_ready"], 1)

                def rotate(t):
                    dve.wait_ge(s["trig_ready"], t + 1)
                    ch(dve.tensor_tensor(prods[:, 0:2, :].rearrange("p c (f n) -> p (c f) n", n=HK),
                                         cs[:, :, :].rearrange("p c (f n) -> p (c f) n", n=HK),
                                         p_t[:, :].unsqueeze(1).to_broadcast([P, 2 * NF, HK]), ALU.mult))
                    dve.wait_ge(s["gprod_ready"], t + 1)
                    ch(dve.tensor_reduce(sums[:, :, :].rearrange("p c n -> p (c n)"),
                                         prods[:, :, :].rearrange("p c (n k) -> p (c n) k", k=K), AX.X, ALU.add))
                    ch.add(dve.tensor_tensor(cs_a[:, :, :], sums[:, 2:4, :], cos1[:, :, :].to_broadcast([P, 2, NF * H]), ALU.mult))
                    ch(dve.tensor_tensor(cs_b[:, :, :], sums[:, 2:4, :], sin1[:, :, :].to_broadcast([P, 2, NF * H]), ALU.mult))
                    ch(dve.tensor_tensor(cs_a[:, :, :], cs_a[:, :, :], sums[:, 0:2, :], ALU.add))
                    ch.add(dve.tensor_tensor(cosw[:, :], cs_a[:, 0, :], cs_b[:, 1, :], ALU.subtract))
                    ch(dve.tensor_tensor(sinw[:, :], cs_a[:, 1, :], cs_b[:, 0, :], ALU.add))
                    ch(dve.tensor_scalar(nsinw[:, :], sinw[:, :], -1.0, None, ALU.mult))
                    dve.wait_ge(s["qk_copied"], t + 1)

                    def per_head(a):
                        return a[:, :].rearrange("p (f h) -> p h f", h=H)

                    def halves(a):
                        return a[:, :].rearrange("p (n h e f) -> p n h e f", n=2, e=2, f=NF)

                    for n in range(2):
                        ch.add(dve.tensor_tensor(halves(rot_a)[:, n], halves(qk)[:, n],
                                                 per_head(cosw).unsqueeze(2).to_broadcast([P, H, 2, NF]), ALU.mult))
                    for e, w in ((0, nsinw), (1, sinw)):
                        ch.add(dve.tensor_tensor(halves(rot_b)[:, :, :, e, :], halves(qk)[:, :, :, 1 - e, :],
                                                 per_head(w).unsqueeze(1).to_broadcast([P, 2, H, NF]), ALU.mult))
                    ch.wait()
                    dve.tensor_tensor(qkr[:, :], rot_a[:, :], rot_b[:, :], ALU.add).then_inc(s["roped"], 1)

                def largest_squares(t):
                    dve.wait_ge(s["sq_ready"], t + 1)
                    ch(dve.tensor_reduce(sq_head[:, :], rot_a[:, :].rearrange("p (n d) -> p n d", d=HD), AX.X, ALU.add))
                    ch(dve.tensor_reduce(sq_tile[:, :], sq_head[:, :], AX.X, ALU.max))
                    dve.tensor_tensor(sq_max[:, :], sq_max[:, :], sq_tile[:, :], ALU.max).then_inc(s["sq_max_ready"], 1)

                def node_softmax(t, first):
                    dve.wait_ge(s["vr_copied"], t * 2 + 2)
                    lv = logit[:, :].rearrange("p (h k) -> p h k", k=K)
                    ch(dve.tensor_reduce(small[:, :], lv, AX.X, ALU.max))
                    dve.tensor_tensor(lv, lv, small[:, :].unsqueeze(2).to_broadcast([P, H, K]), ALU.subtract).then_inc(s["lg_shifted"], 1)
                    dve.wait_ge(s["p_exped"], t + 1)
                    ev = lexp[:, :].rearrange("p (h k) -> p h k", k=K)
                    ch(dve.tensor_reduce(small[:, :], ev, AX.X, ALU.add))
                    ch(dve.reciprocal(small[:, :], small[:, :]))
                    if not first:
                        dve.wait_ge(s["p_saved"], t)
                    dve.tensor_tensor(p_t[:, :].rearrange("p (h k) -> p h k", k=K), ev,
                                      small[:, :].unsqueeze(2).to_broadcast([P, H, K]), ALU.mult).then_inc(s["p_ready"], 1)

                def positions(t):
                    dve.wait_ge(s["pos_ps"], t + 1)
                    dve.tensor_scalar(pos[:, :], side[0][:, 0:HK], 0.0, float(MAX_POS), ALU.max, ALU.min).then_inc(s["pos_taken"], 1)
                    dve.wait_ge(s["p_ready"], t + 1)
                    ch(dve.tensor_tensor(acc[:, :], acc[:, :], p_t[:, :], ALU.add))
                    ch.add(dve.tensor_scalar(acc[:, :], acc[:, :], carry[:, bass.ds(t + 1, 1)], None, ALU.mult))
                    dve.wait_ge(s["pos_taken"], t + 1)
                    ch(dve.tensor_copy(pos_i[:, :], pos[:, :]))
                    ch(dve.tensor_copy(base_t[:, :], pos_i[:, :]))
                    ch(dve.tensor_tensor(over_t[:, :], base_t[:, :], pos[:, :], ALU.is_gt))
                    dve.tensor_tensor(base_t[:, :], base_t[:, :], over_t[:, :], ALU.subtract).then_inc(s["pf_ready"], 1)
                    dve.wait_ge(s["pf_ready"], t + 1)
                    ch(dve.tensor_tensor(pos[:, :], pos[:, :], base_t[:, :], ALU.subtract))
                    dve.tensor_tensor(g_t[:, :], pos[:, :], p_t[:, :], ALU.mult).then_inc(s["g_ready"], 1)
                    dve.wait_ge(s["theta_ready"], t + 1)
                    th = theta[:, :, :].rearrange("p f n -> p (f n)")
                    ch(dve.tensor_scalar(whole[:, :], th, 0.5 / PI, ROUND, ALU.mult, ALU.add))
                    ch(dve.tensor_scalar(whole[:, :], whole[:, :], -ROUND, None, ALU.add))
                    ch(dve.scalar_tensor_tensor(out=angle[:, :], in0=whole[:, :], scalar=-TWO_PI_HI, in1=th, op0=ALU.mult, op1=ALU.add))
                    dve.scalar_tensor_tensor(out=angle[:, :], in0=whole[:, :], scalar=-TWO_PI_LO, in1=angle[:, :],
                                             op0=ALU.mult, op1=ALU.add).then_inc(s["angle_ready"], 1)

                def split(t):
                    dve.wait_ge(s["qkT_ps"], t + 1)
                    dve.wait_ge(s["part_stored"], t * 64 + 64)
                    ch(dve.tensor_reduce(sq_top[:, :], side[0][0:1, 3 * P:4 * P], AX.X, ALU.max))
                    dve.tensor_scalar(bounded[:, bass.ds(t, 1)], sq_top[:, :], LIMIT, None, ALU.is_le).then_inc(s["bounded_ready"], 1)
                    v = side[1][:, :].rearrange("p (n c) -> p n c", c=P)
                    dve.wait_ge(s["bounded_ready"], t + 2)
                    ch(dve.tensor_copy(parts[:, :, 0, :], v))
                    dve.tensor_tensor(rest[:, :, :], v, parts[:, :, 0, :], ALU.subtract).then_inc(s["rest_ready"], 1)

                def mix_nodes(i, c):
                    dve.wait_ge(s["av_done"], i * NU + last_of[c] + 1 + PRIME_E)
                    pp = of_head(prob, i, K)[:, c * CH:(c + 1) * CH, :]
                    dve.tensor_tensor(mixed[:, :, :, :], mix[c % 2][:, 0:CH * K * VW].rearrange("p (t k w) -> p t k w", t=CH, k=K),
                                      pp.unsqueeze(3).to_broadcast([P, CH, K, VW]), ALU.mult).then_inc(s["u_taken"], 1)
                    dve.wait_ge(s["u_taken"], i * NC + c + 1 + PRIME_U)
                    ch(dve.tensor_reduce(summed[:, :, :], mixed[:, :, :, :].rearrange("p t k w -> p t w k"), AX.X, ALU.add))
                    ch(dve.reciprocal(recip[:, :], summed[:, :, HD]))
                    dve.tensor_tensor(of_head(vo, i, HD)[:, c * CH:(c + 1) * CH, :], summed[:, :, 0:HD],
                                      recip[:, :].unsqueeze(2).to_broadcast([P, CH, HD]), ALU.mult).then_inc(s["o_ready"], 1)

                def maxima(i):
                    for n, (t, a, w) in enumerate(pieces):
                        dve.wait_ge(s["max_ps"], i * NP + n + 1)
                        src = ring[n % 2][:, :, :].rearrange("p b n -> p (b n)")[:, 0:w]
                        dve.tensor_reduce(top[:, n:n + 1], src, AX.X, ALU.max).then_inc(s["max_taken"], 1)
                    dve.wait_ge(s["max_taken"], i * NP + NP + PRIME_M)
                    one = sum(1 for (t, a, w) in pieces if (t + 1) * P <= 1024)
                    dve.tensor_scalar(ntop[:, 0:one], top[:, 0:one], -1.0, None, ALU.mult).then_inc(s["max_step"], 1)
                    two = top[:, one:NP].rearrange("p (t n) -> p t n", n=2)
                    dve.tensor_tensor(ntop[:, one:TB], two[:, :, 0], two[:, :, 1], ALU.max).then_inc(s["max_step"], 1)
                    dve.wait_ge(s["max_step"], i * 3 + 2)
                    dve.tensor_scalar(ntop[:, one:TB], ntop[:, one:TB], -1.0, None, ALU.mult).then_inc(s["top_ready"], 1)
                    dve.wait_ge(s["topT_ps"], i + 1)
                    dve.wait_ge(s["shift_loaded"], i * 32 + 32)
                    dve.tensor_copy(shift[:, 0, :], side[1][0:TB, 0:P]).then_inc(s["max_step"], 1)
                    dve.wait_ge(s["max_step"], i * 3 + 3)
                    dve.tensor_tensor(shift[:, 1, :], side[1][0:TB, 0:P], shift[:, 0, :], ALU.subtract).then_inc(s["shift_ready"], 1)

                def add_residual(t):
                    dve.wait_ge(s["post_ps"], t + 1)
                    dve.wait_ge(s["res_loaded"], t * 16 + 16)
                    dve.wait_ge(s["out_stored"], t * 16 + 16)
                    dve.tensor_tensor(yout[:, :], side[0][:, 0:D], xres[:, :], ALU.add).then_inc(s["post_summed"], 1)

                def find_maxima(j, fin):
                    with dve.If(scores_bounded(dve, fin) < 1):
                        maxima(j)
                    with dve.Else():
                        dve.sem_inc(s["max_taken"], NP)
                        dve.sem_inc(s["max_step"], 3)
                        dve.sem_inc(s["top_ready"], 1)
                        dve.sem_inc(s["shift_ready"], 1)

                def run(ip, q, new=None, fin=None, head=None, post=None):
                    if head is not None:
                        mix_nodes(head, 0)
                    if fin is not None:
                        rotate(fin)
                    if head is not None:
                        mix_nodes(head, 1)
                    if fin is not None:
                        largest_squares(fin)
                    first = isinstance(new, int) and new == 0
                    last = is_last(new, T)
                    if new is not None:
                        if not last:
                            gather_statistics(new + 1)
                        node_softmax(new, first)
                        if not last:
                            statistics(new + 1)
                    if head is not None:
                        mix_nodes(head, 2)
                    if new is not None:
                        positions(new)
                    if fin is not None:
                        split(fin)
                    if new is not None and not last:
                        normalise(new + 1)
                    if head is not None:
                        if not is_last(head, HEADS):
                            find_maxima(head + 1, fin)
                        mix_nodes(head, 3)
                    if post is not None:
                        add_residual(post)

                gather_statistics(0)
                ch.wait()
                statistics(0)
                normalise(0, True)
                def steps(new=False, fin=False, head=False):
                    return (18 if new else 0) + (16 if fin else 0) + (8 if head else 0)

                run(0, 0, new=0)
                start = ch.base + ch.n
                with dve.Fori(1, LEAD) as t:
                    ch.at(start, t - 1, steps(True, True))
                    run(0, 0, new=t, fin=t - 1)
                ch.after(start, LEAD - 1, steps(True, True))
                find_maxima(0, TB)
                start, per = ch.base, 2 * steps(True, True, True)
                with dve.Fori(0, LEAD // 2) as ip:
                    ch.at(start, ip, per)
                    for q in range(2):
                        i = ip * 2 + q
                        run(ip, q, new=i + LEAD, fin=i + LEAD - 1, head=i)
                ch.after(start, LEAD // 2, per)
                start = ch.base
                lo, hi = LEAD // 2, (HEADS - LEAD) // 2 - 1
                with dve.Fori(lo, hi) as ip:
                    ch.at(start, ip - lo, per)
                    for q in range(2):
                        i = ip * 2 + q
                        run(ip, q, new=i + LEAD, fin=i + LEAD - 1, head=i, post=i - LEAD)
                ch.after(start, hi - lo, per)
                for i in range(HEADS - LEAD - 2, HEADS - LEAD + 2):
                    run(i // 2, i % 2, new=i + LEAD if i + LEAD < T else None,
                        fin=i + LEAD - 1 if i + LEAD - 1 < T else None, head=i, post=i - LEAD)
                start, per = ch.base + ch.n, 2 * steps(head=True)
                lo, hi = (HEADS - LEAD) // 2 + 1, HEADS // 2 - 1
                with dve.Fori(lo, hi) as ip:
                    ch.at(start, ip - lo, per)
                    for q in range(2):
                        i = ip * 2 + q
                        run(ip, q, head=i, post=i - LEAD)
                ch.after(start, hi - lo, per)
                for i in (HEADS - 2, HEADS - 1):
                    run(i // 2, i % 2, head=i, post=i - LEAD)
                with dve.Fori(HEADS - LEAD, T) as t:
                    run(0, 0, post=t)

            @block.tensor
            def _(pe):
                pe.sem_inc(s["av_done"], PRIME_E)
                pe.wait_ge(s["consts_ready"], 1)
                pe.wait_ge(s["w_scaled"], 1)

                def scores(i, q, u):
                    c, j, t0 = units[u]
                    pe.wait_ge(s["exp_ready"], i * NU + u + 1)
                    for n in range(2):
                        w = 512 - t0 * P
                        out = ring[u % 2][:, n, :] if t0 == 0 else ring[u % 2][:, 0, n * w:(n + 1) * w]
                        t = j + n - CH * c
                        lastm = pe.matmul(out, kT[q][:, (j + n) * P:(j + n + 1) * P],
                                          qT[q][:, c * 512 + t0 * P:(c + 1) * 512], start=True, stop=(t < 0))
                        if t >= 0:
                            lastm = pe.matmul(out[:, (t - t0) * P:(t - t0 + 1) * P], ident_b[:, :], late_kq[:, :],
                                              start=False, stop=True)
                    lastm.then_inc(s["s_ps"], 1)

                def weighted(i, q, u):
                    c, j, t0 = units[u]
                    pe.wait_ge(s["exp_ready"], i * NU + u + 1 + PRIME_S)
                    begin = u == 0 or units[u - 1][0] != c
                    if begin:
                        pe.wait_ge(s["u_taken"], i * NC + c + 1)
                    for n in range(2):
                        for t in range(max(t0, j + n - CH * c), CH):
                            col = t * P if t0 == 0 else n * 256 + (t - t0) * P
                            e = ew[u % NE_BUF][:, n if t0 == 0 else 0, col:col + P]
                            for h in range(0, P, P // 2):
                                lastm = pe.matmul(mix[c % 2][h:h + P // 2, t * K * VW:(t + 1) * K * VW], e[:, h:h + P // 2],
                                                  val[q][:, j + n, :, :].rearrange("p k w -> p (k w)"),
                                                  start=(begin and n == 0 and t == max(t0, j - CH * c)),
                                                  stop=(u in last_of and n == 1), skip_group_check=True)
                    return lastm

                def score_rows(i, q):
                    pe.wait_ge(s["exp_ready"], i * NU + PRIME_S)
                    for n, (t, a, w) in enumerate(pieces):
                        pe.wait_ge(s["max_taken"], i * NP + n + 1)
                        for b in range(0, w, 512):
                            wb = min(512, w - b)
                            end = a + b + wb == (t + 1) * P
                            lastm = pe.matmul(ring[n % 2][:, b // 512, 0:wb], qT[q][0:KQ, t * P:(t + 1) * P],
                                              kT[q][0:KQ, a + b:a + b + wb], start=True, stop=not end)
                            if end:
                                lastm = pe.matmul(ring[n % 2][:, b // 512, wb - P:wb], ident_b[:, :], late_qk[:, :],
                                                  start=False, stop=True)
                        lastm.then_inc(s["max_ps"], 1)
                    pe.wait_ge(s["top_ready"], i + 1)
                    pe.transpose(side[1][0:TB, 0:P], ntop[:, :], ident[:, :]).then_inc(s["topT_ps"], 1)

                def begin_head(ip, q, j, fin):
                    need_none = scores_bounded(pe, fin)
                    pe.wait_ge(qk_loaded[q], ip * 96 + 96)
                    with pe.If(need_none < 1):
                        score_rows(j, q)
                        pe.wait_ge(s["shift_loaded"], j * 32 + 64)
                    with pe.Else():
                        pe.sem_inc(s["max_ps"], NP)
                        pe.sem_inc(s["topT_ps"], 1)

                def run(ip, q, new=None, fin=None, head=None, post=None):
                    first = isinstance(new, int) and new == 0

                    def turn():
                        if new is not None:
                            pe.wait_ge(s["xn_ready"], new + 1)
                            if not first:
                                pe.wait_ge(s["pos_taken"], new)
                        elif post is not None:
                            pe.wait_ge(s["pos_taken"], T)
                        if post is not None:
                            pe.wait_ge(s["o_staged"], post + 1)
                            pe.wait_ge(s["post_summed"], post + 1)
                        if fin is not None:
                            pe.wait_ge(s["bounded_ready"], fin + 1)
                        elif head is not None:
                            pe.wait_ge(s["bounded_ready"], T + 1)
                        if new is not None:
                            for k in range(DK):
                                lastm = pe.transpose(side[0][:, k * P:(k + 1) * P], xn[:, k * P:(k + 1) * P], ident[:, :])
                            lastm.then_inc(s["xnT_ps"], 1)
                        if post is not None:
                            for k in range(DK):
                                lastm = pe.transpose(side[0][:, (2 + k) * P:(3 + k) * P], ostage[:, k * P:(k + 1) * P], ident[:, :])
                            lastm.then_inc(s["oT_ps"], 1)

                    def turned_count():
                        return new + 1 if new is not None else post + 1 + 2 * LEAD

                    def project():
                        if new is None:
                            return
                        pe.wait_ge(s["turned_ready"], turned_count())
                        if fin is not None and not (isinstance(fin, int) and fin == 0):
                            pe.wait_ge(s["rest_ready"], fin)
                        for k in range(DK):
                            pe.matmul(side[1][:, :], turned[:, k, :], w_all[:, k, 0:2 * D], start=(k == 0), stop=(k == DK - 1))
                        for k in range(DK):
                            lastm = pe.matmul(side[0][:, 0:D + HK], turned[:, k, :], w_all[:, k, 2 * D:],
                                              start=(k == 0), stop=(k == DK - 1))
                        lastm.then_inc(s["qkv_ps"], 1)

                    def sums_before():
                        if new is not None:
                            pe.wait_ge(s["vr_copied"], new * 2 + 2)
                        elif post is not None:
                            pe.wait_ge(s["turned_ready"], turned_count())
                        if fin is not None:
                            pe.wait_ge(s["sq_max_ready"], fin + 1)
                            pe.transpose(side[0][0:1, 3 * P:4 * P], sq_max[:, :], ident[:, :])
                        if new is not None:
                            pe.wait_ge(s["p_ready"], new + 1)
                            pe.matmul(side[0][:, 0:HK], before[:, :], p_t[:, :], start=True, stop=False)
                            pe.matmul(side[0][:, 0:HK], ones[:, :], acc[:, :], start=False, stop=True).then_inc(s["pos_ps"], 1)
                        if fin is not None:
                            pe.wait_ge(s["roped"], fin + 1)
                            pe.wait_ge(s["qk_copied"], new + 1 if new is not None else T)
                            for n in range(4):
                                lastm = pe.transpose(side[1][:, n * P:(n + 1) * P], qkr[:, n * P:(n + 1) * P], ident[:, :])
                            lastm.then_inc(s["qkT_ps"], 1)

                    def output():
                        if post is None:
                            return
                        pe.wait_ge(s["turned_ready"], turned_count())
                        if new is not None:
                            pe.wait_ge(s["pos_taken"], new + 1)
                        if fin is not None:
                            pe.wait_ge(s["bounded_ready"], fin + 2)
                        for k in range(DK):
                            lastm = pe.matmul(side[0][:, 0:D], turned[:, 2 + k, :], wo[:, k, :], start=(k == 0), stop=(k == DK - 1))
                        lastm.then_inc(s["post_ps"], 1)

                    if head is None:
                        turn()
                        project()
                        sums_before()
                        output()
                        return
                    pe.wait_ge(s["val_ready"], head * 2 + 2)
                    for u in range(NU):
                        if u + 2 < NU:
                            scores(head, q, u + 2)
                        elif not is_last(head, HEADS):
                            if u + 2 == NU:
                                begin_head(ip + q, 1 - q, head + 1, fin)
                            scores(head + 1, 1 - q, u + 2 - NU)
                        weighted(head, q, u).then_inc(s["av_done"], 1)
                        if u == 2:
                            turn()
                        if u == 6:
                            project()
                        if u == 13:
                            sums_before()
                        if u == 18:
                            output()

                def first_head():
                    begin_head(0, 0, 0, TB)
                    for u in range(2):
                        scores(0, 0, u)

                schedule(pe, run, first_head)


def macaron_block(nc, x, Wq, Wk, Wv, Wr, Wo, gate_w, w1, w2, out):
    B, S, _ = x.shape
    x = x.rearrange("b s d -> (b s) d")
    out = out.rearrange("b s d -> (b s) d")
    N = x.shape[0]
    heads, width = 16, Wq.shape[1] // 16
    table = nc.dram_tensor("table", [N, D + w1.shape[0]], F32).ap()
    q_parts = nc.dram_tensor("q_parts", [B * heads, width, 3, S], BF16).ap()
    k_parts = nc.dram_tensor("k_parts", [B * heads, width, 3, S], BF16).ap()
    build_ffn(nc, "ffn1", x, out, True, gate_w, w1, w2, table)
    build_attention(nc, out, Wq, Wk, Wv, Wr, Wo, q_parts, k_parts, B)
    build_ffn(nc, "ffn2", out, out, False, gate_w, w1, w2, table)


_INS = ['L0_attn_x', 'L0_attn_Wq', 'L0_attn_Wk', 'L0_attn_Wv', 'L0_attn_Wr', 'L0_attn_Wo', 'L0_ffn_gate_w', 'L0_ffn_w1', 'L0_ffn_w2']
_OUTS = [((4, 2048, 256), 'float32')]


def kernel(**inputs):
    import numpy as _np
    import concourse.bacc as _bacc
    from concourse import mybir as _mybir
    from concourse.bass_utils import run_bass_kernel_spmd as _run

    nc = _bacc.Bacc("TRN2", target_bir_lowering=False, num_devices=1)
    arrays, args = {}, []
    for name in _INS:
        a = _np.ascontiguousarray(inputs[name])
        arrays[f"in_{name}_dram"] = a
        args.append(nc.dram_tensor(f"in_{name}_dram", a.shape, _mybir.dt.from_np(a.dtype), kind="ExternalInput").ap())
    for i, (shape, dtype) in enumerate(_OUTS):
        dt = _mybir.dt.from_np(_np.dtype(dtype))
        args.append(nc.dram_tensor(f"out_{i}_dram", shape, dt, kind="ExternalOutput").ap())
    macaron_block(nc, *args)
    r = _run(nc, [arrays], core_ids=[0])
    got = tuple(r.results[0][f"out_{i}_dram"] for i in range(len(_OUTS)))
    return got[0]
```

```python
import concourse.bass as bass
from concourse import mybir
from contextlib import ExitStack

import numpy as np

F32 = mybir.dt.float32
BF16 = mybir.dt.bfloat16
I32 = mybir.dt.int32
ALU = mybir.AluOpType
ACT = mybir.ActivationFunctionType
AX = mybir.AxisListType

P = 128
D = 256
DK = D // P
LN_EPS = 1e-5


class Chain:

    def __init__(self, eng, sem):
        self.eng, self.sem, self.base, self.n = eng, sem, 0, 0

    def __call__(self, ins):
        self.add(ins)
        self.wait()

    def add(self, ins):
        ins.then_inc(self.sem, 1)
        self.n += 1

    def wait(self):
        self.eng.wait_ge(self.sem, self.base + self.n)

    def at(self, start, i, per):
        self.base, self.n = start + i * per, 0

    def after(self, start, count, per):
        assert self.n == per, (self.n, per)
        self.base, self.n = start + count * per, 0


def identity(pool, chain, tile, n=P):
    chain(pool.memset(tile, 0.0))
    chain(pool.affine_select(out=tile, in_=tile, compare_op=ALU.not_equal, fill=1.0,
                             base=0, pattern=[[-1, n]], channel_multiplier=1))


def build_ffn(nc, name, src, dst, residual, gate_w, w1, w2, table):
    N = src.shape[0]
    T = N // P
    NE, F, _ = w1.shape
    FK = F // P
    CAP = -(-N // NE)
    J = CAP // P
    SLOT_LO = 32
    SLOT_HI = CAP // SLOT_LO
    ROW = table.shape[1]
    GT = 4
    G = T // GT
    XB = 4
    THRESHOLD = 0.9
    NOT_CHOSEN = -16.0
    SEARCH = 28
    STEPS = 14
    assert (T, NE, DK, FK, SLOT_HI) == (64, 8, 2, 2, 32)

    with ExitStack() as ctx:
        def sb(n, shape, dt=F32):
            return ctx.enter_context(nc.sbuf_tensor(f"{name}_{n}", shape, dt))

        def sem(n):
            return ctx.enter_context(nc.semaphore(f"{name}_{n}"))

        pair = [ctx.enter_context(nc.psum_tensor(f"{name}_pair{i}", [P, 2, 512], F32)) for i in range(2)]
        bank = [ctx.enter_context(nc.psum_tensor(f"{name}_bank{i}", [P, 512], F32)) for i in range(4)]
        ident = sb("ident", [P, P])
        ones = sb("ones", [P, P], BF16)
        before = sb("before", [P, P], BF16)
        count_i = sb("count_i", [P, T], I32)
        count_b = sb("count_b", [P, T], BF16)
        part_i = sb("part_i", [P, 1], I32)
        part = sb("part", [P, 1])
        gate_in = sb("gate_in", [NE, D])
        gateT = sb("gateT", [P, DK, NE])
        xin = [sb(f"xin{b}", [P, GT, D]) for b in range(XB)]
        xn = [sb(f"xn{q}", [P, GT, D]) for q in range(2)]
        xnT = [sb(f"xnT{q}", [P, DK, GT * P]) for q in range(2)]
        stats = [sb(f"stats{q}", [P, GT, 6]) for q in range(2)]
        mv = [sb(f"mv{q}", [P, GT, 2]) for q in range(2)]
        var = [sb(f"var{q}", [P, GT]) for q in range(2)]
        std = [sb(f"std{q}", [P, GT]) for q in range(2)]
        rstd = [sb(f"rstd{q}", [P, GT]) for q in range(2)]
        prob = sb("prob", [P, NE, T])
        work = sb("work", [P, NE, T])
        first = [sb(f"first{q}", [P, NE, T]) for q in range(2)]
        rank = sb("rank", [P, NE, T])
        csum = sb("csum", [P, NE, T])
        order = sb("order", [P, NE, T])
        score = sb("score", [P, T, NE])
        row_t = sb("row_t", [P, T])
        hit = sb("hit", [P, NE, T], BF16)
        count = sb("count", [P, NE], BF16)
        low = sb("low", [P, NE])
        cand = sb("cand", [P, NE])
        step = [sb(f"step{q}", [P, 1]) for q in range(2)]
        got = sb("got", [P, NE])
        need = sb("need", [P, NE])
        onesT = sb("onesT", [P, T])
        through = sb("through", [P, NE, T])
        place = sb("place", [P, NE, T])
        keep = sb("keep", [P, NE, T])
        place_i = sb("place_i", [P, NE, T], I32)
        digit_i = sb("digit_i", [P, NE, T], I32)
        hi = sb("hi", [P, NE, T], BF16)
        lo = sb("lo", [P, NE, T], BF16)
        pick_hi = [sb(f"pick_hi{q}", [P, T, SLOT_HI], BF16) for q in range(2)]
        pick_lo = [sb(f"pick_lo{q}", [P, T, 2 * SLOT_LO], BF16) for q in range(2)]
        tile_of = sb("tile_of", [SLOT_HI, SLOT_LO])
        idx_hi = sb("idx_hi", [SLOT_HI, NE, SLOT_LO], I32)
        idx_all = sb("idx_all", [P, NE * J], I32)
        rows = [sb(f"rows{q}", [P, J, ROW]) for q in range(2)]
        w1_in = [sb(f"w1_in{q}", [P, FK, D]) for q in range(2)]
        w2_in = [sb(f"w2_in{q}", [P, DK, F]) for q in range(2)]
        w1T = [sb(f"w1T{q}", [P, DK, F]) for q in range(2)]
        w2T = [sb(f"w2T{q}", [P, FK, D]) for q in range(2)]
        xeT = sb("xeT", [P, DK, CAP])
        hT = sb("hT", [P, FK, CAP])
        slot_score = [sb(f"slot_score{q}", [P, J]) for q in range(2)]
        y = [sb(f"y{q}", [P, J, D]) for q in range(2)]

        residual_copied = sem("residual_copied")
        consts_ready = sem("consts_ready")
        pool_step = sem("pool_step")
        dve_step = sem("dve_step")
        gate_loaded = sem("gate_loaded")
        gateT_ps = sem("gateT_ps")
        gateT_ready = sem("gateT_ready")
        x_loaded = [sem(f"x_loaded{b}") for b in range(XB)]
        var_ready = sem("var_ready")
        std_ready = sem("std_ready")
        xn_ready = sem("xn_ready")
        xn_stored = [sem(f"xn_stored{q}") for q in range(2)]
        xnT_ps = sem("xnT_ps")
        xnT_ready = sem("xnT_ready")
        logits_ps = sem("logits_ps")
        logits_ready = sem("logits_ready")
        shifted = sem("shifted")
        exped = sem("exped")
        front_ready = sem("front_ready")
        ranked = sem("ranked")
        score_ready = sem("score_ready")
        score_stored = sem("score_stored")
        count_ready = sem("count_ready")
        total_ps = sem("total_ps")
        mask_ready = sem("mask_ready")
        prefix_ps = sem("prefix_ps")
        picks_ready = sem("picks_ready")
        idx_ps = sem("idx_ps")
        idx_hi_ready = sem("idx_hi_ready")
        idx_moved = sem("idx_moved")
        w_loaded = [sem(f"w_loaded{q}") for q in range(2)]
        gathered = [sem(f"gathered{q}") for q in range(2)]
        turned_ps = sem("turned_ps")
        turned = sem("turned")
        h_ps = sem("h_ps")
        h_ready = sem("h_ready")
        y_ps = sem("y_ps")
        y_ready = sem("y_ready")
        slot_score_ready = sem("slot_score_ready")
        added = sem("added")

        src_g = src.rearrange("(g t p) d -> g p t d", t=GT, p=P)
        table_x = table[:, 0:D].rearrange("(g t p) d -> g p t d", t=GT, p=P)
        table_s = table[:, D:D + NE].rearrange("(t p) e -> p t e", p=P)
        w1_v = w1.rearrange("e (k p) d -> e p k d", p=P)
        w2_v = w2.rearrange("e (k p) f -> e p k f", p=P)
        idx_ps_bank = bank[0]

        def over_t(a):
            return a.unsqueeze(2).to_broadcast([P, NE, T])

        def over_e(a, n=NE):
            return a.unsqueeze(1).to_broadcast([P, n, T])

        with nc.Block() as block:

            @block.sync
            def _(sp):
                sp.dma_start(gate_in[:, :], gate_w).then_inc(gate_loaded, 16)
                for b in range(XB):
                    sp.dma_start(xin[b][:, :, :], src_g[b]).then_inc(x_loaded[b], 16)

                def store_load(g, b, load):
                    sp.wait_ge(xn_ready, g + 1)
                    sp.dma_start(table_x[g], xn[b % 2][:, :, :]).then_inc(xn_stored[b % 2], 16)
                    if load:
                        sp.dma_start(xin[b][:, :, :], src_g[g + XB]).then_inc(x_loaded[b], 16)

                with sp.Fori(0, G // XB - 1) as gb:
                    for b in range(XB):
                        store_load(gb * XB + b, b, True)
                for b in range(XB):
                    store_load(G - XB + b, b, False)
                for q in range(2):
                    sp.dma_start(w1_in[q][:, :, :], w1_v[q]).then_inc(w_loaded[q], 16)
                    sp.dma_start(w2_in[q][:, :, :], w2_v[q]).then_inc(w_loaded[q], 16)
                if residual:
                    sp.dma_start(dst, src).then_inc(residual_copied, 16)
                sp.wait_ge(score_ready, 1)
                sp.dma_start(table_s, score[:, :, :]).then_inc(score_stored, 16)

                def move_idx(e):
                    sp.wait_ge(idx_hi_ready, e + 1)
                    sp.dma_start(idx_all[:, e * J:(e + 1) * J],
                                 idx_hi[:, e, :].rearrange("a (c j) -> a c j", j=J)).then_inc(idx_moved, 16)

                move_idx(0)
                sp.wait_ge(idx_moved, 16)
                move_idx(1)
                for e in range(NE - 2):
                    q = e % 2
                    sp.wait_ge(turned_ps, e * 3 + 1)
                    sp.dma_start(w1_in[q][:, :, :], w1_v[e + 2]).then_inc(w_loaded[q], 16)
                    sp.dma_start(w2_in[q][:, :, :], w2_v[e + 2]).then_inc(w_loaded[q], 16)
                    sp.wait_ge(idx_moved, e * 16 + 32)
                    move_idx(e + 2)

            @block.gpsimd
            def _(pool):
                ch = Chain(pool, pool_step)
                identity(pool, ch, ident[:, :])
                ch(pool.memset(before[:, :], 1.0))
                ch(pool.affine_select(out=before[:, :], in_=before[:, :], compare_op=ALU.is_gt, fill=0.0,
                                      base=0, pattern=[[1, P]], channel_multiplier=-1))
                pool.memset(ones[:, :], 1.0).then_inc(consts_ready, 1)
                ch(pool.iota(count_i[:, :], [[1, T]], base=0, channel_multiplier=0))
                ch(pool.iota(part_i[:, :], [[0, 1]], base=0, channel_multiplier=1))
                ch(pool.tensor_copy(count_b[:, :], count_i[:, :]))
                pool.tensor_copy(part[:, :], part_i[:, :]).then_inc(consts_ready, 1)

                ch(pool.memset(rank[:, :, :], 1.0))
                for o in range(NE):
                    pool.wait_ge(front_ready, o + 1)
                    if o >= 1:
                        pool.wait_ge(ranked, o)
                    pool.tensor_tensor(rank[:, :, :], rank[:, :, :], first[o % 2][:, :, :], ALU.add).then_inc(ranked, 1)

                def gather(e):
                    if e >= 2:
                        pool.wait_ge(turned_ps, (e - 1) * 3)
                        pool.wait_ge(slot_score_ready, e - 1)
                    pool.wait_ge(idx_moved, 16 * (e + 1))
                    for j in range(J):
                        pool.indirect_dma_start(
                            out=rows[e % 2][:, j, :], out_offset=None, in_=table,
                            in_offset=bass.IndirectOffsetOnAxis(ap=idx_all[:, e * J + j:e * J + j + 1], axis=0),
                        ).then_inc(gathered[e % 2], 16)

                def scatter(e):
                    if e >= 1:
                        pool.wait_ge(added, e * J * 16)
                    pool.wait_ge(y_ready, e * J + J)
                    for j in range(J):
                        pool.indirect_dma_start(
                            out=dst, out_offset=bass.IndirectOffsetOnAxis(ap=idx_all[:, e * J + j:e * J + j + 1], axis=0),
                            in_=y[e % 2][:, j, :], in_offset=None, compute_op=ALU.add,
                        ).then_inc(added, 16)

                pool.wait_ge(score_stored, 16)
                for q in range(2):
                    pool.wait_ge(xn_stored[q], 16 * (G // 2))
                gather(0)
                gather(1)
                if residual:
                    pool.wait_ge(residual_copied, 16)
                for e in range(NE):
                    if e + 2 < NE:
                        gather(e + 2)
                    scatter(e)
                pool.wait_ge(added, NE * J * 16)

            @block.scalar
            def _(act):
                act.wait_ge(gateT_ps, 1)
                act.activation(gateT[:, :, :], bank[0][:, 0:DK * NE].rearrange("p (k e) -> p k e", k=DK),
                               ACT.Copy).then_inc(gateT_ready, 1)

                def normalise(gp, start):
                    for q in range(2):
                        g = gp * 2 + q
                        act.wait_ge(var_ready, g + 1)
                        act.activation(std[q][:, :], var[q][:, :], ACT.Sqrt).then_inc(std_ready, 1)
                    for q in range(2):
                        g = gp * 2 + q
                        act.wait_ge(xnT_ps, g + 1)
                        if not start:
                            act.wait_ge(logits_ps, g - 1)
                        act.activation(xnT[q][:, :, :], pair[q][:, :, :], ACT.Copy).then_inc(xnT_ready, 1)

                normalise(0, True)
                with act.Fori(1, G // 2) as gp:
                    normalise(gp, False)
                act.wait_ge(shifted, 1)
                act.activation(prob[:, :, :], work[:, :, :], ACT.Exp).then_inc(exped, 1)

                def expert(ep, q, start):
                    e = ep * 2 + q
                    ring = [pair[(3 * q + s) % 2] for s in range(3)]
                    act.wait_ge(turned_ps, e * 3 + 1)
                    if not start:
                        act.wait_ge(y_ps, e * J - J)
                    act.activation(w1T[q][:, :, :], ring[0][:, 0, :].rearrange("p (k f) -> p k f", k=DK), ACT.Copy)
                    act.activation(w2T[q][:, :, :], ring[0][:, 1, :].rearrange("p (k d) -> p k d", k=FK),
                                   ACT.Copy).then_inc(turned, 1)
                    for s in range(2):
                        act.wait_ge(turned_ps, e * 3 + 2 + s)
                        if s == 0 and (not start or q):
                            act.wait_ge(h_ps, e * 4)
                        act.activation(xeT[:, :, s * 512:(s + 1) * 512], ring[1 + s][:, :, :],
                                       ACT.Copy).then_inc(turned, 1)
                    if not start or q:
                        act.wait_ge(y_ps, e * J)
                    for s in range(2):
                        for f in range(FK):
                            n = 2 * s + f
                            act.wait_ge(h_ps, e * 4 + n + 1)
                            act.activation(hT[:, f, s * 512:(s + 1) * 512], bank[n % 2][:, :],
                                           ACT.Gelu).then_inc(h_ready, 1)

                for q in range(2):
                    expert(0, q, True)
                with act.Fori(1, NE // 2) as ep:
                    for q in range(2):
                        expert(ep, q, False)

            @block.vector
            def _(dve):
                ch = Chain(dve, dve_step)
                dve.wait_ge(consts_ready, 2)
                ch(dve.memset(onesT[:, :], 1.0))

                def statistics(gb, h):
                    for q in range(2):
                        b = 2 * h + q
                        dve.wait_ge(x_loaded[b], gb * 16 + 16)
                        for t in range(GT):
                            ch.add(dve.bn_stats(stats[q][:, t, :], xin[b][:, t, :]))
                        if q == 0:
                            ch.wait()
                    for q in range(2):
                        for t in range(GT):
                            ch.add(dve.bn_aggr(mv[q][:, t, :], stats[q][:, t, :]))
                        ch.wait()
                        dve.tensor_scalar(var[q][:, :], mv[q][:, :, 1], LN_EPS, None, ALU.add).then_inc(var_ready, 1)

                def scale(gp, h, q, start):
                    g = gp * 2 + q
                    dve.wait_ge(std_ready, g + 1)
                    ch(dve.reciprocal(rstd[q][:, :], std[q][:, :]))
                    if not start:
                        dve.wait_ge(xnT_ps, g - 1)
                        dve.wait_ge(xn_stored[q], gp * 16)
                    for t in range(GT):
                        last = dve.tensor_scalar(xn[q][:, t, :], xin[2 * h + q][:, t, :], mv[q][:, t, 0:1],
                                                 rstd[q][:, t:t + 1], ALU.subtract, ALU.mult)
                    last.then_inc(xn_ready, 1)

                def take_logits(gp, q):
                    g = gp * 2 + q
                    dve.wait_ge(logits_ps, g + 1)
                    dve.tensor_copy(prob[:, :, bass.ds(g * GT, GT)],
                                    bank[q][:, 0:GT * NE].rearrange("p (t e) -> p e t", t=GT)).then_inc(logits_ready, 1)

                base = ch.n
                per = 2 * (2 * GT + 1)

                def pair_of_groups(gb, h, start):
                    gp = gb * (XB // 2) + h
                    statistics(gb, h)
                    for q in range(2):
                        scale(gp, h, q, start)
                    if not start:
                        for q in range(2):
                            take_logits(gp - 1, q)

                for h in range(XB // 2):
                    pair_of_groups(0, h, h == 0)
                per *= XB // 2
                with dve.Fori(1, G // XB) as gb:
                    ch.at(base, gb, per)
                    for h in range(XB // 2):
                        pair_of_groups(gb, h, False)
                ch.after(base, G // XB, per)
                for q in range(2):
                    take_logits(G // 2 - 1, q)
                dve.wait_ge(logits_ready, G)

                def by_t(a):
                    return a[:, :, :].rearrange("p e t -> p t e")

                ch(dve.tensor_reduce(row_t[:, :], by_t(prob), AX.X, ALU.max))
                dve.tensor_tensor(work[:, :, :], prob[:, :, :], over_e(row_t[:, :]), ALU.subtract).then_inc(shifted, 1)
                dve.wait_ge(exped, 1)
                ch(dve.tensor_reduce(row_t[:, :], by_t(prob), AX.X, ALU.add))
                ch(dve.reciprocal(row_t[:, :], row_t[:, :]))
                ch(dve.tensor_tensor(prob[:, :, :], prob[:, :, :], over_e(row_t[:, :]), ALU.mult))

                ch(dve.memset(csum[:, :, :], 0.0))
                for o in range(NE):
                    front = first[o % 2]
                    if o >= 2:
                        dve.wait_ge(ranked, o - 1)
                    ch.add(dve.memset(front[:, o, :], 0.0))
                    if o > 0:
                        last = dve.tensor_tensor(front[:, 0:o, :], over_e(prob[:, o, :], o), prob[:, 0:o, :], ALU.is_gt)
                        if o < NE - 1:
                            ch.add(last)
                    if o < NE - 1:
                        last = dve.tensor_tensor(front[:, o + 1:, :], over_e(prob[:, o, :], NE - 1 - o),
                                                 prob[:, o + 1:, :], ALU.is_ge)
                    last.then_inc(front_ready, 1)
                    ch.wait()
                    dve.wait_ge(front_ready, o + 1)
                    ch(dve.tensor_tensor(through[:, :, :], front[:, :, :], over_e(prob[:, o, :]), ALU.mult))
                    ch.add(dve.tensor_tensor(csum[:, :, :], csum[:, :, :], through[:, :, :], ALU.add))
                ch.wait()
                dve.wait_ge(ranked, NE)
                chosen = first[0]
                ch(dve.tensor_scalar(chosen[:, :, :], csum[:, :, :], THRESHOLD, None, ALU.is_lt))
                ch(dve.tensor_tensor(work[:, :, :], prob[:, :, :], chosen[:, :, :], ALU.mult))
                dve.tensor_scalar(score[:, :, :], work[:, :, :].rearrange("p e t -> p t e"), 0.5, None,
                                  ALU.mult).then_inc(score_ready, 1)
                ch(dve.tensor_tensor(order[:, :, :], prob[:, :, :], rank[:, :, :], ALU.subtract))
                ch.add(dve.tensor_tensor(order[:, :, :], order[:, :, :], chosen[:, :, :], ALU.mult))
                ch(dve.tensor_scalar(work[:, :, :], chosen[:, :, :], -NOT_CHOSEN, NOT_CHOSEN, ALU.mult, ALU.add))
                ch(dve.tensor_tensor(order[:, :, :], order[:, :, :], work[:, :, :], ALU.add))

                def count_hits(threshold, op):
                    ch(dve.tensor_tensor(hit[:, :, :], order[:, :, :], over_t(threshold), op))
                    with nc.allow_low_precision("counts up to T are exact"):
                        dve.tensor_reduce(count[:, :], hit[:, :, :], AX.X, ALU.add).then_inc(count_ready, 1)

                ch(dve.memset(low[:, :], NOT_CHOSEN))
                ch(dve.memset(step[0][:, :], -NOT_CHOSEN / 2))
                start = ch.n + ch.base
                with dve.Fori(0, SEARCH // STEPS) as sb4:
                    ch.at(start, sb4, 5 * STEPS)
                    for n in range(STEPS):
                        ch(dve.tensor_scalar(cand[:, :], low[:, :], step[n % 2][:, 0:1], None, ALU.add))
                        count_hits(cand[:, :], ALU.is_ge)
                        ch.add(dve.tensor_scalar(step[1 - n % 2][:, :], step[n % 2][:, :], 0.5, None, ALU.mult))
                        dve.wait_ge(total_ps, sb4 * STEPS + n + 1)
                        ch(dve.tensor_scalar(got[:, :], bank[2][:, 0:NE], float(CAP), step[n % 2][:, 0:1], ALU.is_ge, ALU.mult))
                        ch(dve.tensor_tensor(low[:, :], low[:, :], got[:, :], ALU.add))
                ch.after(start, SEARCH // STEPS, 5 * STEPS)
                count_hits(low[:, :], ALU.is_gt)
                dve.wait_ge(total_ps, SEARCH + 1)
                ch(dve.tensor_scalar(need[:, :], bank[2][:, 0:NE], -1.0, float(CAP), ALU.mult, ALU.add))
                ch(dve.tensor_copy(keep[:, :, :], hit[:, :, :]))
                dve.tensor_tensor(hit[:, :, :], order[:, :, :], over_t(low[:, :]), ALU.is_equal).then_inc(mask_ready, 1)

                def places(n):
                    dve.wait_ge(prefix_ps, n)
                    tiles = bank[3][:, :].rearrange("p (e t) -> p e t", e=NE)
                    for e in range(NE):
                        ch.add(dve.tensor_tensor_scan(through[:, e, :], onesT[:, :], tiles[:, e, :], 0.0, ALU.mult, ALU.add))
                    ch.wait()
                    ch(dve.tensor_tensor(through[:, :, :], through[:, :, :], tiles, ALU.subtract))
                    ch(dve.tensor_tensor(place[:, :, :], through[:, :, :],
                                         bank[2][:, :].rearrange("p (e t) -> p e t", e=NE), ALU.add))

                dve.wait_ge(mask_ready, 1)
                places(1)
                ch(dve.tensor_tensor(work[:, :, :], place[:, :, :], over_t(need[:, :]), ALU.is_lt))
                ch(dve.tensor_tensor(work[:, :, :], work[:, :, :], hit[:, :, :], ALU.mult))
                ch(dve.tensor_tensor(keep[:, :, :], keep[:, :, :], work[:, :, :], ALU.add))
                dve.tensor_copy(hit[:, :, :], keep[:, :, :]).then_inc(mask_ready, 1)
                places(2)
                ch(dve.tensor_copy(place_i[:, :, :], place[:, :, :]))
                ch(dve.tensor_scalar(digit_i[:, :, :], place_i[:, :, :], SLOT_LO - 1, None, ALU.bitwise_and))
                ch(dve.tensor_copy(lo[:, :, :], digit_i[:, :, :]))
                ch(dve.tensor_scalar(digit_i[:, :, :], place_i[:, :, :], SLOT_LO.bit_length() - 1, None,
                                     ALU.logical_shift_right))
                ch(dve.tensor_copy(work[:, :, :], digit_i[:, :, :]))
                ch(dve.tensor_scalar(work[:, :, :], work[:, :, :], 1.0, None, ALU.add))
                ch(dve.tensor_tensor(work[:, :, :], work[:, :, :], keep[:, :, :], ALU.mult))
                ch(dve.tensor_scalar(hi[:, :, :], work[:, :, :], -1.0, None, ALU.add))

                shape = [P, T, SLOT_LO]
                digits = count_b[:, 0:SLOT_LO].unsqueeze(1).to_broadcast(shape)

                def take_idx(ep, q):
                    e = ep * 2 + q
                    dve.wait_ge(idx_ps, e + 1)
                    ch(dve.tensor_copy(tile_of[:, :], idx_ps_bank[0:SLOT_HI, SLOT_LO:2 * SLOT_LO]))
                    dve.scalar_tensor_tensor(
                        out=idx_hi[:, bass.ds(e, 1), :].rearrange("a e l -> a (e l)"),
                        in0=tile_of[:, :], scalar=float(P),
                        in1=idx_ps_bank[0:SLOT_HI, 0:SLOT_LO], op0=ALU.mult, op1=ALU.add).then_inc(idx_hi_ready, 1)

                def picks(ep, q, start):
                    e = ep * 2 + q
                    if not start:
                        dve.wait_ge(idx_ps, e - 1)

                    def of(a):
                        return a[:, bass.ds(e, 1), :].rearrange("p e t -> p (e t)").unsqueeze(2).to_broadcast(shape)

                    dve.tensor_tensor(pick_hi[q][:, :, :], digits, of(hi), ALU.is_equal).then_inc(picks_ready, 1)
                    ch(dve.tensor_tensor(pick_lo[q][:, :, 0:SLOT_LO], digits, of(lo), ALU.is_equal))
                    ch(dve.tensor_tensor(pick_lo[q][:, :, SLOT_LO:], pick_lo[q][:, :, 0:SLOT_LO],
                                         count_b[:, :].unsqueeze(2).to_broadcast(shape), ALU.mult))
                    dve.tensor_scalar(pick_lo[q][:, :, 0:SLOT_LO], pick_lo[q][:, :, 0:SLOT_LO], part[:, 0:1], None,
                                      ALU.mult).then_inc(picks_ready, 1)

                def expert(ep, q, start):
                    e = ep * 2 + q
                    dve.wait_ge(gathered[q], ep * (16 * J) + 16 * J)
                    if not start:
                        dve.wait_ge(added, e * (J * 16) - J * 16)
                    dve.tensor_copy(slot_score[q][:, :], rows[q][:, :, bass.ds(e + D, 1)].rearrange("p j e -> p (j e)")
                                    ).then_inc(slot_score_ready, 1)
                    dve.wait_ge(slot_score_ready, e + 1)
                    for j in range(J):
                        dve.wait_ge(y_ps, e * J + j + 1)
                        dve.tensor_scalar(y[q][:, j, :], bank[2 + j % 2][:, 0:D],
                                          slot_score[q][:, j:j + 1], None, ALU.mult).then_inc(y_ready, 1)

                def steps(ep, q, start, ahead):
                    if ahead:
                        picks(ep + 1, q, False)
                    expert(ep, q, start)
                    if ahead:
                        take_idx(ep + 1, q)

                picks(0, 0, True)
                picks(0, 1, True)
                take_idx(0, 0)
                take_idx(0, 1)
                for q in range(2):
                    steps(0, q, True, True)
                start, per = ch.base + ch.n, 2 * 3
                with dve.Fori(1, NE // 2 - 1) as ep:
                    ch.at(start, ep - 1, per)
                    for q in range(2):
                        steps(ep, q, False, True)
                ch.after(start, NE // 2 - 2, per)
                for q in range(2):
                    steps(NE // 2 - 1, q, False, False)

            @block.tensor
            def _(pe):
                pe.wait_ge(consts_ready, 2)
                pe.wait_ge(gate_loaded, 16)
                for k in range(DK):
                    last = pe.transpose(bank[0][:, k * NE:(k + 1) * NE], gate_in[:, k * P:(k + 1) * P], ident[0:NE, 0:NE])
                last.then_inc(gateT_ps, 1)
                pe.wait_ge(gateT_ready, 1)

                def normalise(gp, start):
                    for q in range(2):
                        g = gp * 2 + q
                        pe.wait_ge(xn_ready, g + 1)
                        if not start:
                            pe.wait_ge(xnT_ready, g - 1)
                        for t in range(GT):
                            for k in range(DK):
                                last = pe.transpose(pair[q][:, k, t * P:(t + 1) * P], xn[q][:, t, k * P:(k + 1) * P],
                                                    ident[:, :])
                        last.then_inc(xnT_ps, 1)
                    for q in range(2):
                        g = gp * 2 + q
                        pe.wait_ge(xnT_ready, g + 1)
                        if not start:
                            pe.wait_ge(logits_ready, g - 1)
                        for t in range(GT):
                            for k in range(DK):
                                last = pe.matmul(bank[q][:, t * NE:(t + 1) * NE], xnT[q][:, k, t * P:(t + 1) * P],
                                                 gateT[:, k, :], start=(k == 0), stop=(k == DK - 1))
                        last.then_inc(logits_ps, 1)

                normalise(0, True)
                with pe.Fori(1, G // 2) as gp:
                    normalise(gp, False)

                with pe.Fori(0, SEARCH + 1) as s:
                    pe.wait_ge(count_ready, s + 1)
                    pe.matmul(bank[2][:, 0:NE], ones[:, :], count[:, :], start=True, stop=True).then_inc(total_ps, 1)
                for n in range(2):
                    pe.wait_ge(mask_ready, n + 1)
                    mask = hit[:, :, :].rearrange("p e t -> p (e t)")
                    pe.matmul(bank[2][:, :], before[:, :], mask, start=True, stop=True)
                    pe.matmul(bank[3][:, :], ones[:, :], mask, start=True, stop=True).then_inc(prefix_ps, 1)

                def slots(ep, q, start):
                    e = ep * 2 + q
                    pe.wait_ge(picks_ready, e * 2 + 2)
                    if not start or q:
                        pe.wait_ge(idx_hi_ready, e)
                    if not start:
                        pe.wait_ge(h_ready, e * 4 - 4)
                    for t in range(T):
                        last = pe.matmul(idx_ps_bank[0:SLOT_HI, 0:2 * SLOT_LO], pick_hi[q][:, t, :], pick_lo[q][:, t, :],
                                         start=(t == 0), stop=(t == T - 1))
                    last.then_inc(idx_ps, 1)

                for q in range(2):
                    slots(0, q, True)

                def expert(ep, q, start, final=False):
                    e = ep * 2 + q
                    ring = [pair[(3 * q + s) % 2] for s in range(3)]

                    def free(s):
                        if not start or 3 * q + s >= 2:
                            pe.wait_ge(turned, e * 3 + s - 1)

                    pe.wait_ge(w_loaded[q], ep * 32 + 32)
                    free(0)
                    for k in range(DK):
                        for f in range(FK):
                            pe.transpose(ring[0][:, 0, (k * FK + f) * P:(k * FK + f + 1) * P],
                                         w1_in[q][:, f, k * P:(k + 1) * P], ident[:, :])
                    for f in range(FK):
                        for k in range(DK):
                            last = pe.transpose(ring[0][:, 1, (f * DK + k) * P:(f * DK + k + 1) * P],
                                                w2_in[q][:, k, f * P:(f + 1) * P], ident[:, :])
                    last.then_inc(turned_ps, 1)
                    pe.wait_ge(gathered[q], ep * (16 * J) + 16 * J)
                    for s in range(2):
                        free(1 + s)
                        for t in range(J // 2):
                            for k in range(DK):
                                last = pe.transpose(ring[1 + s][:, k, t * P:(t + 1) * P],
                                                    rows[q][:, s * (J // 2) + t, k * P:(k + 1) * P], ident[:, :])
                        last.then_inc(turned_ps, 1)
                    pe.wait_ge(idx_hi_ready, NE if final else e + 2)
                    for s in range(2):
                        pe.wait_ge(turned, e * 3 + 2 + s)
                        for f in range(FK):
                            n = 2 * s + f
                            if not start or q or n >= 2:
                                pe.wait_ge(h_ready, e * 4 + n - 1)
                            for k in range(DK):
                                last = pe.matmul(bank[n % 2][:, :], w1T[q][:, k, f * P:(f + 1) * P],
                                                 xeT[:, k, s * 512:(s + 1) * 512], start=(k == 0), stop=(k == DK - 1))
                            last.then_inc(h_ps, 1)
                    for j in range(J):
                        pe.wait_ge(h_ready, e * 4 + (2 if j < J // 2 else 4))
                        if not start or q or j >= 2:
                            pe.wait_ge(y_ready, e * J + j - 1)
                        for f in range(FK):
                            last = pe.matmul(bank[2 + j % 2][:, 0:D], hT[:, f, j * P:(j + 1) * P],
                                             w2T[q][:, f, :], start=(f == 0), stop=(f == FK - 1))
                        last.then_inc(y_ps, 1)

                for q in range(2):
                    expert(0, q, True)
                    slots(1, q, False)
                with pe.Fori(1, NE // 2 - 1) as ep:
                    for q in range(2):
                        expert(ep, q, False)
                        slots(ep + 1, q, False)
                for q in range(2):
                    expert(NE // 2 - 1, q, False, final=True)


def build_attention(nc, x, Wq, Wk, Wv, Wr, Wo, q_parts, k_parts, B):
    N = x.shape[0]
    S = N // B
    TB = S // P
    T = N // P
    H, K = 16, Wr.shape[1] // 16
    HD = D // H
    NF = HD // 2
    HK = H * K
    VW = HD + 1
    EPS = 1e-8
    HALF_SCALE = HD ** -0.25
    LIMIT = 40.0
    MAX_POS = 2048 - 1
    ROPE_BASE = 10000.0
    PARTS = 3
    KQ = 6 * HD
    KS = KQ + 2
    Q_ROWS = [(0, 3, 0), (3, 2, 0), (5, 1, 0)]
    K_ROWS = [(0, 3, 0), (3, 2, 1), (5, 1, 2)]
    CH = 4
    NC = TB // CH
    HEADS = B * H
    LEAD = TB + 2
    NEG = -1e30
    ROUND = 1.5 * 2.0 ** 23
    PI = float(np.pi)
    TWO_PI_HI = 6.28125
    TWO_PI_LO = 2.0 * PI - TWO_PI_HI
    freq = [float(f) for f in np.float32(1.0) / np.float32(ROPE_BASE) ** (np.arange(0, HD, 2, dtype=np.float32) / HD)]
    assert (TB, H, K, NC, HEADS) == (16, 16, 4, 4, T)

    units = []
    for c in range(NC):
        units += [(c, 2 * p, 0) for p in range(2 * c)] + [(c, CH * c, 0), (c, CH * c + 2, 2)]
    NU = len(units)
    last_of = [max(u for u in range(NU) if units[u][0] == c) for c in range(NC)]
    pieces = [(t, a, min(1024, (t + 1) * P - a)) for t in range(TB) for a in range(0, (t + 1) * P, 1024)]
    NP = len(pieces)

    with ExitStack() as ctx:
        def sb(n, shape, dt=F32):
            return ctx.enter_context(nc.sbuf_tensor(f"at_{n}", shape, dt))

        def sem(n):
            return ctx.enter_context(nc.semaphore(f"at_{n}"))

        ring = [ctx.enter_context(nc.psum_tensor(f"at_ring{i}", [P, 2, 512], F32)) for i in range(2)]
        mix = [ctx.enter_context(nc.psum_tensor(f"at_mix{i}", [P, 512], F32)) for i in range(2)]
        side = [ctx.enter_context(nc.psum_tensor(f"at_side{i}", [P, 512], F32)) for i in range(2)]

        ident = sb("ident", [P, P])
        ident_b = sb("ident_b", [P, P], BF16)
        ones = sb("ones", [P, P])
        before = sb("before", [P, P])
        late_kq = sb("late_kq", [P, P], BF16)
        late_qk = sb("late_qk", [P, P], BF16)
        sq_max = sb("sq_max", [P, 1])
        sq_top = sb("sq_top", [1, 1])
        sq_tile = sb("sq_tile", [P, 1])
        sq_head = sb("sq_head", [P, 2 * H])
        bounded = sb("bounded", [1, T], I32)
        freq_t = sb("freq_t", [P, NF, HK])
        cos1 = sb("cos1", [P, 1, NF * H])
        sin1 = sb("sin1", [P, 1, NF * H])
        half_pi = sb("half_pi", [P, 1])
        eps_t = sb("eps_t", [P, 1])
        carry_i = sb("carry_i", [P, T + 1], I32)
        carry = sb("carry", [P, T + 1])
        w_all = sb("w_all", [P, DK, 3 * D + HK])
        wo = sb("wo", [P, DK, D])
        vo = sb("vo", [P, T, D])
        prob = sb("prob", [P, T, HK])
        xin = sb("xin", [P, D])
        stats = sb("stats", [P, 6])
        mv = sb("mv", [P, 2])
        var = sb("var", [P, 1])
        logv = sb("logv", [P, 1])
        rs0 = sb("rs0", [P, 1])
        rs1 = sb("rs1", [P, 1])
        xn = sb("xn", [P, D])
        turned = sb("turned", [P, 4, P])
        qk = sb("qk", [P, 2 * D])
        logit = sb("logit", [P, HK])
        small = sb("small", [P, H])
        lexp = sb("lexp", [P, HK])
        p_t = sb("p_t", [P, HK])
        acc = sb("acc", [P, HK])
        pos = sb("pos", [P, HK])
        pos_i = sb("pos_i", [P, HK], I32)
        base_t = sb("base_t", [P, HK])
        over_t = sb("over_t", [P, HK])
        g_t = sb("g_t", [P, HK])
        theta = sb("theta", [P, NF, HK])
        whole = sb("whole", [P, NF * HK])
        angle = sb("angle", [P, NF * HK])
        angle_abs = sb("angle_abs", [P, NF * HK])
        cs = sb("cs", [P, 2, NF * HK])
        prods = sb("prods", [P, 4, NF * HK])
        sums = sb("sums", [P, 4, NF * H])
        cs_a = sb("cs_a", [P, 2, NF * H])
        cs_b = sb("cs_b", [P, 2, NF * H])
        cosw = sb("cosw", [P, NF * H])
        sinw = sb("sinw", [P, NF * H])
        nsinw = sb("nsinw", [P, NF * H])
        rot_a = sb("rot_a", [P, 2 * D])
        rot_b = sb("rot_b", [P, 2 * D])
        qkr = sb("qkr", [P, 2 * D])
        rest = sb("rest", [P, 4, P])
        parts = sb("parts", [P, 4, PARTS, P], BF16)
        qT = [sb(f"qT{q}", [KS, S], BF16) for q in range(2)]
        kT = [sb(f"kT{q}", [KS, S], BF16) for q in range(2)]
        val = [sb(f"val{q}", [P, TB, K, VW]) for q in range(2)]
        NE_BUF = 4
        ew = [sb(f"ew{n}", [P, 2, 512]) for n in range(NE_BUF)]
        mixed = sb("mixed", [P, CH, K, VW])
        summed = sb("summed", [P, CH, VW])
        recip = sb("recip", [P, CH])
        top = sb("top", [P, NP])
        ntop = sb("ntop", [P, TB])
        shift = sb("shift", [TB, 2, P], BF16)
        ostage = sb("ostage", [P, D])
        xres = [sb(f"xres{q}", [P, D]) for q in range(2)]
        yout = [sb(f"yout{q}", [P, D]) for q in range(2)]

        names = ("consts_ready pool_step dve_step act_step w_loaded w_scaled x_loaded var_ready rs_ready xn_ready xnT_ps "
                 "oT_ps turned_ready qkv_ps qk_copied vr_copied lg_shifted p_exped p_ready p_saved pos_ps pos_taken "
                 "pf_ready angle_ready trig_abs trig_ready g_ready gprod_ready roped qkT_ps rest_ready mid_ready "
                 "lo_ready part_stored s_ps exp_ready av_done u_taken val_ready o_ready max_ps max_taken "
                 "top_ready topT_ps shift_ready shift_loaded sq_ready sq_max_ready bounded_ready max_step o_staged post_ps post_summed").split()
        s = {n: sem(n) for n in names}
        res_loaded = [sem(f"res_loaded{q}") for q in range(2)]
        out_stored = [sem(f"out_stored{q}") for q in range(2)]
        qk_loaded = [sem(f"qk_loaded{q}") for q in range(2)]

        x_v = x.rearrange("(t p) d -> t p d", p=P)
        q_tile = q_parts.rearrange("(b g h) d a s -> b g (h d) a s", b=B, g=2)
        k_tile = k_parts.rearrange("(b g h) d a s -> b g (h d) a s", b=B, g=2)

        def of_head(a, i, w):
            v = a[:, :, :].rearrange("p (b t) (h d) -> p b t h d", b=B, h=H)
            return v[:, bass.ds(i // H, 1), :, bass.ds(i % H, 1), :].rearrange("p b t h d -> p (b t) (h d)")

        def row(a, t):
            return a[:, bass.ds(t, 1), :].rearrange("p t d -> p (t d)")

        PRIME_S, PRIME_U, PRIME_M, PRIME_E = 2, 2, 2, NU + NE_BUF

        def scores_bounded(eng, fin):
            tile = fin - 1 if fin is not None else T - 1
            if fin is None:
                eng.wait_ge(s["bounded_ready"], T + 1)
            return eng.value_load(bounded[0:1, bass.ds(tile, 1)], min_val=0, max_val=1)

        def schedule(eng, run, last_projections, first_head=None):
            run(0, 0, new=0)
            with eng.Fori(1, LEAD) as t:
                run(0, 0, new=t, fin=t - 1)
            if first_head is not None:
                first_head()
            with eng.Fori(0, LEAD // 2) as ip:
                for q in range(2):
                    i = ip * 2 + q
                    run(ip, q, new=i + LEAD, fin=i + LEAD - 1, head=i)
            with eng.Fori(LEAD // 2, (HEADS - LEAD) // 2 - 1) as ip:
                for q in range(2):
                    i = ip * 2 + q
                    run(ip, q, new=i + LEAD, fin=i + LEAD - 1, head=i, post=i - LEAD)
            for i in range(HEADS - LEAD - 2, HEADS - LEAD + 2):
                run(i // 2, i % 2, new=i + LEAD if i + LEAD < T else None,
                    fin=i + LEAD - 1 if i + LEAD - 1 < T else None, head=i, post=i - LEAD)
            with eng.Fori((HEADS - LEAD) // 2 + 1, HEADS // 2 - 1) as ip:
                for q in range(2):
                    i = ip * 2 + q
                    run(ip, q, head=i, post=i - LEAD)
            for i in (HEADS - 2, HEADS - 1):
                run(i // 2, i % 2, head=i, post=i - LEAD)
            with eng.Fori((HEADS - LEAD) // 2, T // 2) as tp:
                last_projections(tp)

        def is_last(i, count):
            return isinstance(i, int) and i == count - 1

        with nc.Block() as block:

            @block.sync
            def _(sp):
                sp.sem_inc(s["part_stored"], 64)
                sp.sem_inc(s["shift_loaded"], 32)
                for q in range(2):
                    sp.sem_inc(out_stored[q], 16)
                for n, (w, o) in enumerate(((Wq, 0), (Wk, D), (Wv, 2 * D), (Wr, 3 * D))):
                    sp.dma_start(w_all[:, :, o:o + w.shape[1]], w.rearrange("(k p) n -> p k n", p=P)).then_inc(s["w_loaded"], 16)
                sp.dma_start(wo[:, :, :], Wo.rearrange("(k p) n -> p k n", p=P)).then_inc(s["w_loaded"], 16)
                sp.dma_start(xin[:, :], x_v[0]).then_inc(s["x_loaded"], 16)

                def load_head(j, q, tiles):
                    if not (isinstance(j, int) and j == 0):
                        sp.wait_ge(s["av_done"], (j - 1) * NU + PRIME_E)
                    sp.wait_ge(s["part_stored"], tiles * 64 + 64)
                    for (dst, src, rows) in ((qT, q_parts, Q_ROWS), (kT, k_parts, K_ROWS)):
                        head = src[bass.ds(j, 1)].rearrange("h d a s -> (h d) a s")
                        for at, n, first in rows:
                            if src is q_parts:
                                part = head[:, first:first + n, :].rearrange("d a s -> a d s")
                            else:
                                part = head[:, first, :].unsqueeze(0).to_broadcast([n, HD, S])
                            sp.dma_start(dst[q][at * HD:(at + n) * HD, :], part).then_inc(qk_loaded[q], 16)

                def load_shift(j, q, fin):
                    with sp.If(scores_bounded(sp, fin) < 1):
                        sp.wait_ge(s["shift_ready"], j + 1)
                        for r in range(2):
                            sp.dma_start(qT[q][KQ + r:KQ + r + 1, :], shift[:, r, :]).then_inc(s["shift_loaded"], 16)
                    with sp.Else():
                        sp.sem_inc(s["shift_loaded"], 32)

                def first_head():
                    load_head(0, 0, TB)
                    load_shift(0, 0, TB)

                def run(ip, q, new=None, fin=None, head=None, post=None):
                    if new is not None and not is_last(new, T):
                        sp.wait_ge(s["xn_ready"], new + 1)
                        sp.dma_start(xin[:, :], x_v[new + 1]).then_inc(s["x_loaded"], 16)
                    if head is not None and not is_last(head, HEADS):
                        load_head(head + 1, 1 - q, head + 1 + TB if fin is not None else T)
                    if post is not None:
                        load_residual(q, post)
                    if fin is not None:
                        sp.wait_ge(s["lo_ready"], fin + 1)
                        for n in range(4):
                            dst = (q_tile, k_tile)[n // 2][fin // TB, n % 2][:, :, bass.ds((fin % TB) * P, P)]
                            sp.dma_start(dst, parts[:, n, :, :]).then_inc(s["part_stored"], 16)
                    if head is not None and not is_last(head, HEADS):
                        load_shift(head + 1, 1 - q, fin)
                    if post is not None:
                        store_output(q, post)

                def load_residual(q, post):
                    sp.wait_ge(s["post_summed"], post + 1)
                    sp.dma_start(xres[q][:, :], x_v[post]).then_inc(res_loaded[q], 16)

                def store_output(q, post):
                    sp.wait_ge(s["post_summed"], post + 3)
                    sp.dma_start(x_v[post], yout[q][:, :]).then_inc(out_stored[q], 16)

                def last_projections(tp):
                    for q in range(2):
                        load_residual(q, tp * 2 + q)
                    for q in range(2):
                        store_output(q, tp * 2 + q)

                schedule(sp, run, last_projections, first_head)
                for q in range(2):
                    sp.wait_ge(out_stored[q], T // 2 * 16 + 16)

            @block.gpsimd
            def _(pool):
                ch = Chain(pool, s["pool_step"])
                identity(pool, ch, ident[:, :])
                ch(pool.tensor_copy(ident_b[:, :], ident[:, :]))
                ch(pool.memset(before[:, :], 1.0))
                ch(pool.affine_select(out=before[:, :], in_=before[:, :], compare_op=ALU.is_gt, fill=0.0,
                                      base=0, pattern=[[1, P]], channel_multiplier=-1))
                for m, a in ((late_kq, 1), (late_qk, -1)):
                    ch(pool.memset(m[:, :], 0.0))
                    ch(pool.affine_select(out=m[:, :], in_=m[:, :], compare_op=ALU.is_ge, fill=NEG,
                                          base=0, pattern=[[a, P]], channel_multiplier=-a))
                ch(pool.memset(ones[:, :], 1.0))
                for f in range(NF):
                    ch(pool.memset(freq_t[:, f, :], freq[f]))
                    ch(pool.memset(cos1[:, :, f * H:(f + 1) * H], float(np.cos(freq[f]) - 1.0)))
                    ch(pool.memset(sin1[:, :, f * H:(f + 1) * H], float(np.sin(freq[f]))))
                ch(pool.memset(half_pi[:, :], PI / 2))
                ch(pool.memset(eps_t[:, :], EPS))
                for q in range(2):
                    ch(pool.memset(qT[q][KQ:KS, :], 0.0))
                    ch(pool.memset(kT[q][KQ:KS, :], 1.0))
                ch(pool.iota(carry_i[:, 0:T], [[0, B], [1, TB]], base=0, channel_multiplier=0))
                ch(pool.memset(carry_i[:, T:T + 1], 0.0))
                ch(pool.tensor_copy(carry[:, :], carry_i[:, :]))
                pool.tensor_scalar(carry[:, :], carry[:, :], 1.0, None, ALU.min).then_inc(s["consts_ready"], 1)

                def stage_outputs(post, outputs):
                    pool.wait_ge(s["o_ready"], outputs)
                    pool.wait_ge(s["oT_ps"], post + 1)
                    pool.tensor_copy(ostage[:, :], row(vo, post)).then_inc(s["o_staged"], 1)

                def last_projections(tp):
                    for q in range(2):
                        stage_outputs(tp * 2 + q, HEADS * NC)

                def weigh_values(j, q, tiles):
                    pool.wait_ge(s["av_done"], (j - 1) * NU + PRIME_E)
                    pool.wait_ge(s["p_saved"], tiles)
                    vv, pp = of_head(vo, j, HD), of_head(prob, j, K)
                    pool.tensor_tensor(val[q][:, :, :, HD], pp, eps_t[:, :].unsqueeze(2).to_broadcast([P, TB, K]),
                                       ALU.add).then_inc(s["val_ready"], 1)
                    pool.wait_ge(s["val_ready"], j * 2 + 1)
                    pool.tensor_tensor(val[q][:, :, :, 0:HD], vv.unsqueeze(2).to_broadcast([P, TB, K, HD]),
                                       val[q][:, :, :, HD].unsqueeze(3).to_broadcast([P, TB, K, HD]),
                                       ALU.mult).then_inc(s["val_ready"], 1)

                def run(ip, q, new=None, fin=None, head=None, post=None):
                    if post is not None:
                        stage_outputs(post, (post + TB) * NC)
                    if head is not None and not is_last(head, HEADS):
                        weigh_values(head + 1, 1 - q, head + 1 + TB if fin is not None else T)
                    if fin is not None:
                        pool.wait_ge(s["trig_ready"], fin + 1)
                        pool.wait_ge(s["g_ready"], fin + 1)
                        pool.tensor_tensor(
                            prods[:, 3, :].rearrange("p (f n) -> p f n", n=HK), cs[:, 1, :].rearrange("p (f n) -> p f n", n=HK),
                            g_t[:, :].unsqueeze(1).to_broadcast([P, NF, HK]), ALU.mult).then_inc(s["gprod_ready"], 1)
                        pool.wait_ge(s["roped"], fin + 1)
                        pool.tensor_tensor(rot_a[:, :], qkr[:, :], qkr[:, :], ALU.mult).then_inc(s["sq_ready"], 1)
                    if new is not None:
                        pool.wait_ge(s["p_ready"], new + 1)
                        pool.tensor_copy(row(prob, new), p_t[:, :]).then_inc(s["p_saved"], 1)
                    if fin is not None:
                        pool.wait_ge(s["mid_ready"], fin + 1)
                        pool.tensor_tensor(parts[:, :, 2, :], rest[:, :, :], parts[:, :, 1, :], ALU.subtract).then_inc(s["lo_ready"], 1)

                schedule(pool, run, last_projections, lambda: weigh_values(0, 0, TB))

            @block.scalar
            def _(act):
                act.wait_ge(s["w_loaded"], 16 * 5)
                act.wait_ge(s["consts_ready"], 1)
                act.sem_inc(s["exp_ready"], PRIME_S)
                act.activation(w_all[:, :, 0:2 * D], w_all[:, :, 0:2 * D], ACT.Copy, scale=HALF_SCALE).then_inc(s["w_scaled"], 1)
                act.preload_act_table_set("natural_log_exp_and_others")

                def rsqrt(t):
                    act.wait_ge(s["var_ready"], t + 1)
                    act.activation(logv[:, :], var[:, :], ACT.Ln).then_inc(s["act_step"], 1)
                    act.wait_ge(s["act_step"], t + 1)
                    act.activation(rs0[:, :], logv[:, :], ACT.Exp, scale=-0.5).then_inc(s["rs_ready"], 1)

                def weights(i, u):
                    c, j, t0 = units[u]
                    w = 512 - t0 * P
                    act.wait_ge(s["s_ps"], i * NU + u + 1)
                    act.wait_ge(s["av_done"], i * NU + u + 1 + NU)
                    out, src = ew[u % NE_BUF], ring[u % 2]
                    if t0 == 0:
                        act.activation(out[:, :, :], src[:, :, :], ACT.Exp).then_inc(s["exp_ready"], 1)
                    else:
                        act.activation(out[:, 0, :], src[:, 0, :], ACT.Exp).then_inc(s["exp_ready"], 1)

                rsqrt(0)

                def run(ip, q, new=None, fin=None, head=None, post=None):
                    start = isinstance(new, int) and new == 0

                    def trig():
                        if fin is None:
                            return
                        act.wait_ge(s["angle_ready"], fin + 1)
                        if not (isinstance(fin, int) and fin == 0):
                            act.wait_ge(s["roped"], fin)
                            act.wait_ge(s["gprod_ready"], fin)
                        act.activation(angle_abs[:, :], angle[:, :], ACT.Abs).then_inc(s["trig_abs"], 1)
                        act.activation(cs[:, 1, :], angle[:, :], ACT.Sin)
                        act.wait_ge(s["trig_abs"], fin + 1)
                        act.activation(cs[:, 0, :], angle_abs[:, :], ACT.Sin, bias=half_pi[:, 0:1], scale=-1.0).then_inc(s["trig_ready"], 1)
                        act.preload_act_table_set("natural_log_exp_and_others")

                    def copy_turned():
                        if new is None and post is None:
                            return
                        a, b = (0 if new is not None else 2), (4 if post is not None else 2)
                        if new is not None:
                            act.wait_ge(s["xnT_ps"], new + 1)
                            if not start:
                                act.wait_ge(s["qkv_ps"], new)
                        if post is not None:
                            act.wait_ge(s["oT_ps"], post + 2)
                            act.wait_ge(s["post_summed"], post + 2)
                        act.activation(turned[:, a:b, :], side[0][:, a * P:b * P].rearrange("p (n c) -> p n c", c=P),
                                       ACT.Copy).then_inc(s["turned_ready"], 1)

                    def copy_qk():
                        if new is None:
                            return
                        act.wait_ge(s["qkv_ps"], new + 1)
                        if not start:
                            act.wait_ge(s["roped"], new)
                        act.activation(qk[:, :], side[1][:, :], ACT.Copy).then_inc(s["qk_copied"], 1)

                    def copy_v_logits():
                        if new is None:
                            return
                        act.wait_ge(s["qkv_ps"], new + 1)
                        if not start:
                            act.wait_ge(s["p_ready"], new)
                        act.activation(row(vo, new), side[0][:, 0:D], ACT.Copy).then_inc(s["vr_copied"], 1)
                        act.activation(logit[:, :], side[0][:, D:D + HK], ACT.Copy).then_inc(s["vr_copied"], 1)

                    def softmax_exp():
                        if new is None:
                            return
                        act.wait_ge(s["lg_shifted"], new + 1)
                        act.activation(lexp[:, :], logit[:, :], ACT.Exp).then_inc(s["p_exped"], 1)

                    def next_rsqrt():
                        if new is not None and not is_last(new, T):
                            rsqrt(new + 1)

                    def middle_part():
                        if fin is None:
                            return
                        act.wait_ge(s["rest_ready"], fin + 1)
                        act.activation(parts[:, :, 1, :], rest[:, :, :], ACT.Copy).then_inc(s["mid_ready"], 1)

                    if head is None:
                        for step in (copy_turned, trig, copy_v_logits, copy_qk, next_rsqrt, softmax_exp, middle_part):
                            step()
                        return
                    side_steps = {4: (copy_turned,), 5: (trig,), 10: (copy_qk, copy_v_logits), 12: (softmax_exp,),
                                  14: (next_rsqrt,), 17: (middle_part,)}
                    for u in range(NU):
                        for step in side_steps.get(u, ()):
                            step()
                        weights(head, u)

                def last_projections(tp):
                    for q in range(2):
                        post, a = tp * 2 + q, 2 - 2 * q
                        act.wait_ge(s["oT_ps"], post + 2)
                        act.wait_ge(s["post_summed"], post + 1)
                        act.activation(turned[:, a:a + 2, :], side[q][:, 0:DK * P].rearrange("p (n c) -> p n c", c=P),
                                       ACT.Copy).then_inc(s["turned_ready"], 1)

                schedule(act, run, last_projections)

            @block.vector
            def _(dve):
                ch = Chain(dve, s["dve_step"])
                dve.sem_inc(s["u_taken"], PRIME_U)
                dve.sem_inc(s["max_taken"], PRIME_M)
                dve.sem_inc(s["post_summed"], 2)
                dve.wait_ge(s["consts_ready"], 1)
                dve.sem_inc(s["bounded_ready"], 1)
                ch(dve.memset(acc[:, :], 0.0))
                ch(dve.memset(sq_max[:, :], 0.0))

                def gather_statistics(t):
                    dve.wait_ge(s["x_loaded"], t * 16 + 16)
                    ch.add(dve.bn_stats(stats[:, :], xin[:, :]))

                def statistics(t):
                    ch(dve.bn_aggr(mv[:, :], stats[:, :]))
                    dve.tensor_scalar(var[:, :], mv[:, 1:2], LN_EPS, None, ALU.add).then_inc(s["var_ready"], 1)

                def normalise(t, first=False):
                    dve.wait_ge(s["rs_ready"], t + 1)
                    ch(dve.tensor_tensor(rs1[:, :], rs0[:, :], rs0[:, :], ALU.mult))
                    ch(dve.tensor_tensor(rs1[:, :], rs1[:, :], var[:, :], ALU.mult))
                    ch(dve.tensor_scalar(rs1[:, :], rs1[:, :], -0.5, 1.5, ALU.mult, ALU.add))
                    ch(dve.tensor_tensor(rs1[:, :], rs1[:, :], rs0[:, :], ALU.mult))
                    if not first:
                        dve.wait_ge(s["xnT_ps"], t)
                    dve.tensor_scalar(xn[:, :], xin[:, :], mv[:, 0:1], rs1[:, 0:1], ALU.subtract, ALU.mult).then_inc(s["xn_ready"], 1)

                def rotate(t):
                    dve.wait_ge(s["trig_ready"], t + 1)
                    dve.tensor_tensor(prods[:, 0:2, :].rearrange("p c (f n) -> p (c f) n", n=HK),
                                      cs[:, :, :].rearrange("p c (f n) -> p (c f) n", n=HK),
                                      p_t[:, :].unsqueeze(1).to_broadcast([P, 2 * NF, HK]), ALU.mult)
                    ch(dve.tensor_tensor(prods[:, 2, :].rearrange("p (f n) -> p f n", n=HK), cs[:, 0, :].rearrange("p (f n) -> p f n", n=HK),
                                         g_t[:, :].unsqueeze(1).to_broadcast([P, NF, HK]), ALU.mult))
                    dve.wait_ge(s["gprod_ready"], t + 1)
                    ch(dve.tensor_reduce(sums[:, :, :].rearrange("p c n -> p (c n)"),
                                         prods[:, :, :].rearrange("p c (n k) -> p (c n) k", k=K), AX.X, ALU.add))
                    ch.add(dve.tensor_tensor(cs_a[:, :, :], sums[:, 2:4, :], cos1[:, :, :].to_broadcast([P, 2, NF * H]), ALU.mult))
                    ch(dve.tensor_tensor(cs_b[:, :, :], sums[:, 2:4, :], sin1[:, :, :].to_broadcast([P, 2, NF * H]), ALU.mult))
                    ch(dve.tensor_tensor(cs_a[:, :, :], cs_a[:, :, :], sums[:, 0:2, :], ALU.add))
                    ch.add(dve.tensor_tensor(cosw[:, :], cs_a[:, 0, :], cs_b[:, 1, :], ALU.subtract))
                    ch(dve.tensor_tensor(sinw[:, :], cs_a[:, 1, :], cs_b[:, 0, :], ALU.add))
                    ch(dve.tensor_scalar(nsinw[:, :], sinw[:, :], -1.0, None, ALU.mult))
                    dve.wait_ge(s["qk_copied"], t + 1)

                    def per_head(a):
                        return a[:, :].rearrange("p (f h) -> p h f", h=H)

                    def halves(a):
                        return a[:, :].rearrange("p (n h e f) -> p n h e f", n=2, e=2, f=NF)

                    for n in range(2):
                        ch.add(dve.tensor_tensor(halves(rot_a)[:, n], halves(qk)[:, n],
                                                 per_head(cosw).unsqueeze(2).to_broadcast([P, H, 2, NF]), ALU.mult))
                    for e, w in ((0, nsinw), (1, sinw)):
                        ch.add(dve.tensor_tensor(halves(rot_b)[:, :, :, e, :], halves(qk)[:, :, :, 1 - e, :],
                                                 per_head(w).unsqueeze(1).to_broadcast([P, 2, H, NF]), ALU.mult))
                    ch.wait()
                    dve.tensor_tensor(qkr[:, :], rot_a[:, :], rot_b[:, :], ALU.add).then_inc(s["roped"], 1)

                def largest_squares(t):
                    dve.wait_ge(s["sq_ready"], t + 1)
                    ch(dve.tensor_reduce(sq_head[:, :], rot_a[:, :].rearrange("p (n d) -> p n d", d=HD), AX.X, ALU.add))
                    ch(dve.tensor_reduce(sq_tile[:, :], sq_head[:, :], AX.X, ALU.max))
                    dve.tensor_tensor(sq_max[:, :], sq_max[:, :], sq_tile[:, :], ALU.max).then_inc(s["sq_max_ready"], 1)

                def node_softmax(t, first):
                    dve.wait_ge(s["vr_copied"], t * 2 + 2)
                    lv = logit[:, :].rearrange("p (h k) -> p h k", k=K)
                    ch(dve.tensor_reduce(small[:, :], lv, AX.X, ALU.max))
                    dve.tensor_tensor(lv, lv, small[:, :].unsqueeze(2).to_broadcast([P, H, K]), ALU.subtract).then_inc(s["lg_shifted"], 1)
                    dve.wait_ge(s["p_exped"], t + 1)
                    ev = lexp[:, :].rearrange("p (h k) -> p h k", k=K)
                    ch(dve.tensor_reduce(small[:, :], ev, AX.X, ALU.add))
                    ch(dve.reciprocal(small[:, :], small[:, :]))
                    if not first:
                        dve.wait_ge(s["p_saved"], t)
                    dve.tensor_tensor(p_t[:, :].rearrange("p (h k) -> p h k", k=K), ev,
                                      small[:, :].unsqueeze(2).to_broadcast([P, H, K]), ALU.mult).then_inc(s["p_ready"], 1)

                def positions(t, fin):
                    dve.wait_ge(s["pos_ps"], t + 1)
                    dve.tensor_scalar(pos[:, :], side[0][:, 0:HK], 0.0, float(MAX_POS), ALU.max, ALU.min).then_inc(s["pos_taken"], 1)
                    if fin is not None:
                        bound(fin)
                    dve.wait_ge(s["p_ready"], t + 1)
                    ch(dve.tensor_tensor(acc[:, :], acc[:, :], p_t[:, :], ALU.add))
                    ch.add(dve.tensor_scalar(acc[:, :], acc[:, :], carry[:, bass.ds(t + 1, 1)], None, ALU.mult))
                    dve.wait_ge(s["pos_taken"], t + 1)
                    ch(dve.tensor_copy(pos_i[:, :], pos[:, :]))
                    ch(dve.tensor_copy(base_t[:, :], pos_i[:, :]))
                    ch(dve.tensor_tensor(over_t[:, :], base_t[:, :], pos[:, :], ALU.is_gt))
                    dve.tensor_tensor(base_t[:, :], base_t[:, :], over_t[:, :], ALU.subtract).then_inc(s["pf_ready"], 1)
                    dve.wait_ge(s["pf_ready"], t + 1)
                    ch.add(dve.tensor_tensor(pos[:, :], pos[:, :], base_t[:, :], ALU.subtract))
                    ch(dve.tensor_tensor(theta[:, :, :], freq_t[:, :, :], base_t[:, :].unsqueeze(1).to_broadcast([P, NF, HK]), ALU.mult))
                    dve.tensor_tensor(g_t[:, :], pos[:, :], p_t[:, :], ALU.mult).then_inc(s["g_ready"], 1)
                    th = theta[:, :, :].rearrange("p f n -> p (f n)")
                    ch(dve.tensor_scalar(whole[:, :], th, 0.5 / PI, ROUND, ALU.mult, ALU.add))
                    ch(dve.tensor_scalar(whole[:, :], whole[:, :], -ROUND, None, ALU.add))
                    ch(dve.scalar_tensor_tensor(out=angle[:, :], in0=whole[:, :], scalar=-TWO_PI_HI, in1=th, op0=ALU.mult, op1=ALU.add))
                    dve.scalar_tensor_tensor(out=angle[:, :], in0=whole[:, :], scalar=-TWO_PI_LO, in1=angle[:, :],
                                             op0=ALU.mult, op1=ALU.add).then_inc(s["angle_ready"], 1)

                def split(t):
                    dve.wait_ge(s["qkT_ps"], t + 1)
                    dve.wait_ge(s["bounded_ready"], t + 1)
                    dve.wait_ge(s["part_stored"], t * 64 + 64)
                    v = side[1][:, :].rearrange("p (n c) -> p n c", c=P)
                    ch(dve.tensor_copy(parts[:, :, 0, :], v))
                    dve.tensor_tensor(rest[:, :, :], v, parts[:, :, 0, :], ALU.subtract).then_inc(s["rest_ready"], 1)

                def bound(t):
                    ch(dve.tensor_reduce(sq_top[:, :], side[0][0:1, 3 * P:4 * P], AX.X, ALU.max))
                    dve.tensor_scalar(bounded[:, bass.ds(t, 1)], sq_top[:, :], LIMIT, None, ALU.is_le).then_inc(s["bounded_ready"], 1)

                def mix_nodes(i, c):
                    dve.wait_ge(s["av_done"], i * NU + last_of[c] + 1 + PRIME_E)
                    pp = of_head(prob, i, K)[:, c * CH:(c + 1) * CH, :]
                    dve.tensor_tensor(mixed[:, :, :, :], mix[c % 2][:, 0:CH * K * VW].rearrange("p (t k w) -> p t k w", t=CH, k=K),
                                      pp.unsqueeze(3).to_broadcast([P, CH, K, VW]), ALU.mult).then_inc(s["u_taken"], 1)
                    dve.wait_ge(s["u_taken"], i * NC + c + 1 + PRIME_U)
                    ch(dve.tensor_reduce(summed[:, :, :], mixed[:, :, :, :].rearrange("p t k w -> p t w k"), AX.X, ALU.add))
                    ch(dve.reciprocal(recip[:, :], summed[:, :, HD]))
                    dve.tensor_tensor(of_head(vo, i, HD)[:, c * CH:(c + 1) * CH, :], summed[:, :, 0:HD],
                                      recip[:, :].unsqueeze(2).to_broadcast([P, CH, HD]), ALU.mult).then_inc(s["o_ready"], 1)

                def maxima(i):
                    for n, (t, a, w) in enumerate(pieces):
                        dve.wait_ge(s["max_ps"], i * NP + n + 1)
                        src = ring[n % 2][:, :, :].rearrange("p b n -> p (b n)")[:, 0:w]
                        dve.tensor_reduce(top[:, n:n + 1], src, AX.X, ALU.max).then_inc(s["max_taken"], 1)
                    dve.wait_ge(s["max_taken"], i * NP + NP + PRIME_M)
                    one = sum(1 for (t, a, w) in pieces if (t + 1) * P <= 1024)
                    dve.tensor_scalar(ntop[:, 0:one], top[:, 0:one], -1.0, None, ALU.mult).then_inc(s["max_step"], 1)
                    two = top[:, one:NP].rearrange("p (t n) -> p t n", n=2)
                    dve.tensor_tensor(ntop[:, one:TB], two[:, :, 0], two[:, :, 1], ALU.max).then_inc(s["max_step"], 1)
                    dve.wait_ge(s["max_step"], i * 3 + 2)
                    dve.tensor_scalar(ntop[:, one:TB], ntop[:, one:TB], -1.0, None, ALU.mult).then_inc(s["top_ready"], 1)
                    dve.wait_ge(s["topT_ps"], i + 1)
                    dve.wait_ge(s["shift_loaded"], i * 32 + 32)
                    dve.tensor_copy(shift[:, 0, :], side[1][0:TB, 0:P]).then_inc(s["max_step"], 1)
                    dve.wait_ge(s["max_step"], i * 3 + 3)
                    dve.tensor_tensor(shift[:, 1, :], side[1][0:TB, 0:P], shift[:, 0, :], ALU.subtract).then_inc(s["shift_ready"], 1)

                def add_residual(tp, q, bank):
                    dve.wait_ge(s["post_ps"], tp * 2 + q + 1)
                    dve.wait_ge(res_loaded[q], tp * 16 + 16)
                    dve.wait_ge(out_stored[q], tp * 16 + 16)
                    dve.tensor_tensor(yout[q][:, :], bank[:, 0:D], xres[q][:, :], ALU.add).then_inc(s["post_summed"], 1)

                def find_maxima(j, fin):
                    with dve.If(scores_bounded(dve, fin) < 1):
                        maxima(j)
                    with dve.Else():
                        dve.sem_inc(s["max_taken"], NP)
                        dve.sem_inc(s["max_step"], 3)
                        dve.sem_inc(s["top_ready"], 1)
                        dve.sem_inc(s["shift_ready"], 1)

                def run(ip, q, new=None, fin=None, head=None, post=None):
                    first = isinstance(new, int) and new == 0
                    last = is_last(new, T)
                    if head is None and new is not None:
                        gather_statistics(new + 1)
                        if fin is not None:
                            rotate(fin)
                        else:
                            ch.wait()
                        statistics(new + 1)
                        if fin is not None:
                            largest_squares(fin)
                        node_softmax(new, first)
                        normalise(new + 1)
                        if fin is not None:
                            split(fin)
                        positions(new, fin)
                        return
                    if head is not None:
                        mix_nodes(head, 0)
                    if fin is not None:
                        rotate(fin)
                    if head is not None:
                        mix_nodes(head, 1)
                    if fin is not None:
                        largest_squares(fin)
                    if new is not None:
                        if not last:
                            gather_statistics(new + 1)
                        node_softmax(new, first)
                        if not last:
                            statistics(new + 1)
                    if head is not None:
                        mix_nodes(head, 2)
                    if fin is not None:
                        split(fin)
                    if new is not None:
                        positions(new, fin)
                    elif fin is not None:
                        bound(fin)
                    if new is not None and not last:
                        normalise(new + 1)
                    if head is not None:
                        if not is_last(head, HEADS):
                            find_maxima(head + 1, fin)
                        mix_nodes(head, 3)
                    if post is not None:
                        add_residual(ip - LEAD // 2, q, side[0])

                gather_statistics(0)
                ch.wait()
                statistics(0)
                normalise(0, True)
                def steps(new=False, fin=False, head=False):
                    return (19 if new else 0) + (16 if fin else 0) + (8 if head else 0)

                run(0, 0, new=0)
                start = ch.base + ch.n
                with dve.Fori(1, LEAD) as t:
                    ch.at(start, t - 1, steps(True, True))
                    run(0, 0, new=t, fin=t - 1)
                ch.after(start, LEAD - 1, steps(True, True))
                find_maxima(0, TB)
                start, per = ch.base, 2 * steps(True, True, True)
                with dve.Fori(0, LEAD // 2) as ip:
                    ch.at(start, ip, per)
                    for q in range(2):
                        i = ip * 2 + q
                        run(ip, q, new=i + LEAD, fin=i + LEAD - 1, head=i)
                ch.after(start, LEAD // 2, per)
                start = ch.base
                lo, hi = LEAD // 2, (HEADS - LEAD) // 2 - 1
                with dve.Fori(lo, hi) as ip:
                    ch.at(start, ip - lo, per)
                    for q in range(2):
                        i = ip * 2 + q
                        run(ip, q, new=i + LEAD, fin=i + LEAD - 1, head=i, post=i - LEAD)
                ch.after(start, hi - lo, per)
                for i in range(HEADS - LEAD - 2, HEADS - LEAD + 2):
                    run(i // 2, i % 2, new=i + LEAD if i + LEAD < T else None,
                        fin=i + LEAD - 1 if i + LEAD - 1 < T else None, head=i, post=i - LEAD)
                start, per = ch.base + ch.n, 2 * steps(head=True)
                lo, hi = (HEADS - LEAD) // 2 + 1, HEADS // 2 - 1
                with dve.Fori(lo, hi) as ip:
                    ch.at(start, ip - lo, per)
                    for q in range(2):
                        i = ip * 2 + q
                        run(ip, q, head=i, post=i - LEAD)
                ch.after(start, hi - lo, per)
                for i in (HEADS - 2, HEADS - 1):
                    run(i // 2, i % 2, head=i, post=i - LEAD)
                with dve.Fori((HEADS - LEAD) // 2, T // 2) as tp:
                    for q in range(2):
                        add_residual(tp, q, side[q])

            @block.tensor
            def _(pe):
                pe.sem_inc(s["av_done"], PRIME_E)
                pe.sem_inc(s["oT_ps"], 1)
                pe.wait_ge(s["consts_ready"], 1)
                pe.wait_ge(s["w_scaled"], 1)

                def scores(i, q, u):
                    c, j, t0 = units[u]
                    pe.wait_ge(s["exp_ready"], i * NU + u + 1)
                    for n in range(2):
                        w = 512 - t0 * P
                        out = ring[u % 2][:, n, :] if t0 == 0 else ring[u % 2][:, 0, n * w:(n + 1) * w]
                        t = j + n - CH * c
                        lastm = pe.matmul(out, kT[q][:, (j + n) * P:(j + n + 1) * P],
                                          qT[q][:, c * 512 + t0 * P:(c + 1) * 512], start=True, stop=(t < 0))
                        if t >= 0:
                            lastm = pe.matmul(out[:, (t - t0) * P:(t - t0 + 1) * P], ident_b[:, :], late_kq[:, :],
                                              start=False, stop=True)
                    lastm.then_inc(s["s_ps"], 1)

                def weighted(i, q, u):
                    c, j, t0 = units[u]
                    pe.wait_ge(s["exp_ready"], i * NU + u + 1 + PRIME_S)
                    begin = u == 0 or units[u - 1][0] != c
                    if begin:
                        pe.wait_ge(s["u_taken"], i * NC + c + 1)
                    for n in range(2):
                        for t in range(max(t0, j + n - CH * c), CH):
                            col = t * P if t0 == 0 else n * 256 + (t - t0) * P
                            e = ew[u % NE_BUF][:, n if t0 == 0 else 0, col:col + P]
                            for h in range(0, P, P // 2):
                                lastm = pe.matmul(mix[c % 2][h:h + P // 2, t * K * VW:(t + 1) * K * VW], e[:, h:h + P // 2],
                                                  val[q][:, j + n, :, :].rearrange("p k w -> p (k w)"),
                                                  start=(begin and n == 0 and t == max(t0, j - CH * c)),
                                                  stop=(u in last_of and n == 1), skip_group_check=True)
                    return lastm

                def score_rows(i, q):
                    pe.wait_ge(s["exp_ready"], i * NU + PRIME_S)
                    for n, (t, a, w) in enumerate(pieces):
                        pe.wait_ge(s["max_taken"], i * NP + n + 1)
                        for b in range(0, w, 512):
                            wb = min(512, w - b)
                            end = a + b + wb == (t + 1) * P
                            lastm = pe.matmul(ring[n % 2][:, b // 512, 0:wb], qT[q][0:KQ, t * P:(t + 1) * P],
                                              kT[q][0:KQ, a + b:a + b + wb], start=True, stop=not end)
                            if end:
                                lastm = pe.matmul(ring[n % 2][:, b // 512, wb - P:wb], ident_b[:, :], late_qk[:, :],
                                                  start=False, stop=True)
                        lastm.then_inc(s["max_ps"], 1)
                    pe.wait_ge(s["top_ready"], i + 1)
                    pe.transpose(side[1][0:TB, 0:P], ntop[:, :], ident[:, :]).then_inc(s["topT_ps"], 1)

                def begin_head(ip, q, j, fin):
                    need_none = scores_bounded(pe, fin)
                    pe.wait_ge(qk_loaded[q], ip * 96 + 96)
                    with pe.If(need_none < 1):
                        score_rows(j, q)
                        pe.wait_ge(s["shift_loaded"], j * 32 + 64)
                    with pe.Else():
                        pe.sem_inc(s["max_ps"], NP)
                        pe.sem_inc(s["topT_ps"], 1)

                def run(ip, q, new=None, fin=None, head=None, post=None):
                    first = isinstance(new, int) and new == 0

                    def turn():
                        if new is not None:
                            pe.wait_ge(s["xn_ready"], new + 1)
                            if not first:
                                pe.wait_ge(s["pos_taken"], new)
                        elif post is not None:
                            pe.wait_ge(s["pos_taken"], T)
                        if post is not None:
                            pe.wait_ge(s["o_staged"], post + 1)
                            pe.wait_ge(s["post_summed"], post + 2)
                        if fin is not None:
                            pe.wait_ge(s["bounded_ready"], fin + 1)
                        elif head is not None:
                            pe.wait_ge(s["bounded_ready"], T + 1)
                        if new is not None:
                            for k in range(DK):
                                lastm = pe.transpose(side[0][:, k * P:(k + 1) * P], xn[:, k * P:(k + 1) * P], ident[:, :])
                            lastm.then_inc(s["xnT_ps"], 1)
                        if post is not None:
                            for k in range(DK):
                                lastm = pe.transpose(side[0][:, (2 + k) * P:(3 + k) * P], ostage[:, k * P:(k + 1) * P], ident[:, :])
                            lastm.then_inc(s["oT_ps"], 1)

                    def turned_count():
                        return new + 1 if new is not None else post + 1 + 2 * LEAD

                    def project():
                        if new is None:
                            return
                        pe.wait_ge(s["turned_ready"], turned_count())
                        if fin is not None and not (isinstance(fin, int) and fin == 0):
                            pe.wait_ge(s["rest_ready"], fin)
                        for k in range(DK):
                            pe.matmul(side[1][:, :], turned[:, k, :], w_all[:, k, 0:2 * D], start=(k == 0), stop=(k == DK - 1))
                        for k in range(DK):
                            lastm = pe.matmul(side[0][:, 0:D + HK], turned[:, k, :], w_all[:, k, 2 * D:],
                                              start=(k == 0), stop=(k == DK - 1))
                        lastm.then_inc(s["qkv_ps"], 1)

                    def sums_before():
                        if new is not None:
                            pe.wait_ge(s["vr_copied"], new * 2 + 2)
                        elif post is not None:
                            pe.wait_ge(s["turned_ready"], turned_count())
                        if fin is not None:
                            pe.wait_ge(s["sq_max_ready"], fin + 1)
                            pe.transpose(side[0][0:1, 3 * P:4 * P], sq_max[:, :], ident[:, :])
                            pe.wait_ge(s["roped"], fin + 1)
                            pe.wait_ge(s["qk_copied"], new + 1 if new is not None else T)
                            for n in range(4):
                                lastm = pe.transpose(side[1][:, n * P:(n + 1) * P], qkr[:, n * P:(n + 1) * P], ident[:, :])
                            lastm.then_inc(s["qkT_ps"], 1)
                        if new is not None:
                            pe.wait_ge(s["p_ready"], new + 1)
                            pe.matmul(side[0][:, 0:HK], before[:, :], p_t[:, :], start=True, stop=False)
                            pe.matmul(side[0][:, 0:HK], ones[:, :], acc[:, :], start=False, stop=True).then_inc(s["pos_ps"], 1)

                    def output():
                        if post is None:
                            return
                        pe.wait_ge(s["turned_ready"], turned_count())
                        if new is not None:
                            pe.wait_ge(s["pos_taken"], new + 1)
                        if fin is not None:
                            pe.wait_ge(s["bounded_ready"], fin + 2)
                        for k in range(DK):
                            lastm = pe.matmul(side[0][:, 0:D], turned[:, 2 + k, :], wo[:, k, :], start=(k == 0), stop=(k == DK - 1))
                        lastm.then_inc(s["post_ps"], 1)

                    if head is None:
                        turn()
                        project()
                        sums_before()
                        return
                    pe.wait_ge(s["val_ready"], head * 2 + 2)
                    for u in range(NU):
                        if u + 2 < NU:
                            scores(head, q, u + 2)
                        elif not is_last(head, HEADS):
                            if u + 2 == NU:
                                begin_head(ip + q, 1 - q, head + 1, fin)
                            scores(head + 1, 1 - q, u + 2 - NU)
                        weighted(head, q, u).then_inc(s["av_done"], 1)
                        if u == 1:
                            turn()
                        if u == 2:
                            project()
                        if u == 12:
                            sums_before()
                        if u == 18:
                            output()

                def first_head():
                    begin_head(0, 0, 0, TB)
                    for u in range(2):
                        scores(0, 0, u)

                def last_projections(tp):
                    for q in range(2):
                        post = tp * 2 + q
                        pe.wait_ge(s["o_staged"], post + 1)
                        pe.wait_ge(s["post_summed"], tp * 2 + 2)
                        for k in range(DK):
                            lastm = pe.transpose(side[q][:, k * P:(k + 1) * P], ostage[:, k * P:(k + 1) * P], ident[:, :])
                        lastm.then_inc(s["oT_ps"], 1)
                    for q in range(2):
                        post, a = tp * 2 + q, 2 - 2 * q
                        pe.wait_ge(s["turned_ready"], post + 1 + 2 * LEAD)
                        for k in range(DK):
                            lastm = pe.matmul(side[q][:, 0:D], turned[:, a + k, :], wo[:, k, :], start=(k == 0), stop=(k == DK - 1))
                        lastm.then_inc(s["post_ps"], 1)

                schedule(pe, run, last_projections, first_head)


def macaron_block(nc, x, Wq, Wk, Wv, Wr, Wo, gate_w, w1, w2, out):
    B, S, _ = x.shape
    x = x.rearrange("b s d -> (b s) d")
    out = out.rearrange("b s d -> (b s) d")
    N = x.shape[0]
    heads, width = 16, Wq.shape[1] // 16
    table = nc.dram_tensor("table", [N, D + w1.shape[0]], F32).ap()
    q_parts = nc.dram_tensor("q_parts", [B * heads, width, 3, S], BF16).ap()
    k_parts = nc.dram_tensor("k_parts", [B * heads, width, 3, S], BF16).ap()
    build_ffn(nc, "ffn1", x, out, True, gate_w, w1, w2, table)
    build_attention(nc, out, Wq, Wk, Wv, Wr, Wo, q_parts, k_parts, B)
    build_ffn(nc, "ffn2", out, out, False, gate_w, w1, w2, table)


_INS = ['L0_attn_x', 'L0_attn_Wq', 'L0_attn_Wk', 'L0_attn_Wv', 'L0_attn_Wr', 'L0_attn_Wo', 'L0_ffn_gate_w', 'L0_ffn_w1', 'L0_ffn_w2']
_OUTS = [((4, 2048, 256), 'float32')]


def kernel(**inputs):
    import numpy as _np
    import concourse.bacc as _bacc
    from concourse import mybir as _mybir
    from concourse.bass_utils import run_bass_kernel_spmd as _run

    nc = _bacc.Bacc("TRN2", target_bir_lowering=False, num_devices=1)
    arrays, args = {}, []
    for name in _INS:
        a = _np.ascontiguousarray(inputs[name])
        arrays[f"in_{name}_dram"] = a
        args.append(nc.dram_tensor(f"in_{name}_dram", a.shape, _mybir.dt.from_np(a.dtype), kind="ExternalInput").ap())
    for i, (shape, dtype) in enumerate(_OUTS):
        dt = _mybir.dt.from_np(_np.dtype(dtype))
        args.append(nc.dram_tensor(f"out_{i}_dram", shape, dt, kind="ExternalOutput").ap())
    macaron_block(nc, *args)
    r = _run(nc, [arrays], core_ids=[0])
    got = tuple(r.results[0][f"out_{i}_dram"] for i in range(len(_OUTS)))
    return got[0]
```
